# Optimizing a Trainium2 kernel written in Bass

```python
import numpy as np
import jax
import jax.numpy as jnp

def _softmax(x, axis=-1):
    return jax.nn.softmax(x, axis=axis)

def _gelu(x):
    return jax.nn.gelu(x, approximate=True)

def _silu(x):
    return jax.nn.silu(x)

def _sigmoid(x):
    return jax.nn.sigmoid(x)

def _layernorm(x, axis=-1, eps=1e-05):
    m = jnp.mean(x, axis=axis, keepdims=True)
    v = jnp.var(x, axis=axis, keepdims=True)
    return (x - m) / jnp.sqrt(v + eps)

def _scatter_add(tgt, idx, src, axis=0):
    return tgt.at[idx].add(src)

def _segment_sum(src, seg, n):
    return jax.ops.segment_sum(src, seg, n)
kernel_name = 'mk_flamingo_gated_d1_seqx_r4_81bc9b'

def setup_inputs(seed: int=0):
    np.random.seed(seed)
    _w = jnp.asarray

    def _rec_inputs():
        import jax
        import jax.numpy as jnp
        _rk = jax.random.key(seed)
        x = 7.22e-05 + 1 * jax.random.normal(jax.random.fold_in(_rk, 1), (4, 1024, 256), jnp.float32)
        _lenS = 1024 - jax.random.randint(jax.random.fold_in(_rk, 7), (4,), 0, max(1, 1024 // 4) + 1, jnp.int32)
        _lenS2 = 154 - jax.random.randint(jax.random.fold_in(_rk, 8), (4,), 0, max(1, 154 // 4) + 1, jnp.int32)
        _ctx_1024P = jax.random.normal(jax.random.fold_in(_rk, 11), (4, 16, 256), jnp.float32)
        _ctx_1024c = jax.random.dirichlet(jax.random.fold_in(_rk, 511), 0.3 * jnp.ones((16,), jnp.float32), (4, 154))
        _ctx_1024t = jnp.einsum('bsk,bkd->bsd', _ctx_1024c, _ctx_1024P)
        _ctx_1024t = _ctx_1024t * jax.lax.rsqrt(jnp.mean(jnp.square(_ctx_1024t)) + 1e-12) * 0.953939
        ctx_1024 = 2.81802e-05 + 1.00001 * (_ctx_1024t + 0.3 * jax.random.normal(jax.random.fold_in(_rk, 611), (4, 154, 256), jnp.float32))
        _g = jax.random.normal(jax.random.fold_in(_rk, 9001), (2, 1), jnp.float32)
        _g = jnp.sign(_g) * jnp.maximum(jnp.abs(_g), 1.0) + (_g == 0) * 1.0
        g_xattn = _g[0]
        g_ffn = _g[1]
        return (x, ctx_1024, g_xattn, g_ffn)
    x, ctx_1024, g_xattn, g_ffn = _rec_inputs()

    def _L0_xattn_setup():
        import jax, jax.numpy as jnp
        import numpy as np
        B, T, S, D = (4, 512, 1024, 256)
        TOP_K = 32

        def _read(query, mem_state, top_k, Wq, bq, Wk, bk, Wv, bv, Wo, bo):
            b, t, d = query.shape
            s = mem_state.shape[1]
            scale = 1.0 / np.sqrt(d)
            q = query @ Wq.T + bq
            k = mem_state @ Wk.T + bk
            v = mem_state @ Wv.T + bv
            scores = jnp.einsum('btd,bsd->bts', q, k) * scale
            if top_k < s:
                vals, idx = jax.lax.top_k(scores, top_k)
                b_ix = jnp.arange(b)[:, None, None]
                t_ix = jnp.arange(t)[None, :, None]
                masked = jnp.full_like(scores, -jnp.inf)
                scores = masked.at[b_ix, t_ix, idx].set(vals)
            attn = jax.nn.softmax(scores, axis=-1)
            ctx = jnp.einsum('bts,bsd->btd', attn, v)
            return ctx @ Wo.T + bo
        key = jax.random.key(seed)
        ks = jax.random.split(key, 12)
        std = 0.02
        inp = {'query': jax.random.normal(ks[0], (B, T, D), dtype=jnp.float32), 'mem_state': jax.random.normal(ks[1], (B, S, D), dtype=jnp.float32), 'top_k': TOP_K, 'Wq': jax.random.normal(ks[2], (D, D), dtype=jnp.float32) * std, 'bq': jnp.zeros((D,), dtype=jnp.float32), 'Wk': jax.random.normal(ks[3], (D, D), dtype=jnp.float32) * std, 'bk': jnp.zeros((D,), dtype=jnp.float32), 'Wv': jax.random.normal(ks[4], (D, D), dtype=jnp.float32) * std, 'bv': jnp.zeros((D,), dtype=jnp.float32), 'Wo': jax.random.normal(ks[5], (D, D), dtype=jnp.float32) * std, 'bo': jnp.zeros((D,), dtype=jnp.float32)}
        return inp
    _L0_xattn_all = _L0_xattn_setup()
    _L0_xattn_in = {k: v for k, v in _L0_xattn_all.items() if k in ('Wq', 'bq', 'Wk', 'bk', 'Wv', 'bv', 'Wo', 'bo')}
    del _L0_xattn_all

    def _L0_ffn_setup():
        import jax, jax.numpy as jnp
        import numpy as np
        HIDDEN = 256
        INTER = 1024
        key = jax.random.key(seed)
        k1, k2, k3, k4, k5 = jax.random.split(key, 5)
        hidden_states = jax.random.normal(k1, (4, 512, HIDDEN), dtype=jnp.float32)
        W1 = jax.random.normal(k2, (HIDDEN, INTER), dtype=jnp.float32) * (1.0 / np.sqrt(HIDDEN))
        b1 = jax.random.normal(k3, (INTER,), dtype=jnp.float32) * 0.02
        W2 = jax.random.normal(k4, (INTER, HIDDEN), dtype=jnp.float32) * (1.0 / np.sqrt(INTER))
        b2 = jax.random.normal(k5, (HIDDEN,), dtype=jnp.float32) * 0.02
        return {'hidden_states': hidden_states, 'W1': W1, 'b1': b1, 'W2': W2, 'b2': b2}
    _L0_ffn_all = _L0_ffn_setup()
    _L0_ffn_in = {k: v for k, v in _L0_ffn_all.items() if k in ('W1', 'b1', 'W2', 'b2')}
    del _L0_ffn_all
    return {'x': x, 'ctx_1024': ctx_1024, 'g_xattn': g_xattn, 'g_ffn': g_ffn, 'L0_xattn_Wq': _L0_xattn_in['Wq'], 'L0_xattn_bq': _L0_xattn_in['bq'], 'L0_xattn_Wk': _L0_xattn_in['Wk'], 'L0_xattn_bk': _L0_xattn_in['bk'], 'L0_xattn_Wv': _L0_xattn_in['Wv'], 'L0_xattn_bv': _L0_xattn_in['bv'], 'L0_xattn_Wo': _L0_xattn_in['Wo'], 'L0_xattn_bo': _L0_xattn_in['bo'], 'L0_ffn_W1': _L0_ffn_in['W1'], 'L0_ffn_b1': _L0_ffn_in['b1'], 'L0_ffn_W2': _L0_ffn_in['W2'], 'L0_ffn_b2': _L0_ffn_in['b2']}

def reference(x, ctx_1024, g_xattn, g_ffn, L0_xattn_Wq, L0_xattn_bq, L0_xattn_Wk, L0_xattn_bk, L0_xattn_Wv, L0_xattn_bv, L0_xattn_Wo, L0_xattn_bo, L0_ffn_W1, L0_ffn_b1, L0_ffn_W2, L0_ffn_b2):
    import jax
    import jax.numpy as jnp

    def _L0_xattn_ref(query, mem_state, top_k, Wq, bq, Wk, bk, Wv, bv, Wo, bo):
        import jax, jax.numpy as jnp
        import numpy as np
        B, T, S, D = (4, 512, 1024, 256)
        TOP_K = 32

        def _read(query, mem_state, top_k, Wq, bq, Wk, bk, Wv, bv, Wo, bo):
            b, t, d = query.shape
            s = mem_state.shape[1]
            scale = 1.0 / np.sqrt(d)
            q = query @ Wq.T + bq
            k = mem_state @ Wk.T + bk
            v = mem_state @ Wv.T + bv
            scores = jnp.einsum('btd,bsd->bts', q, k) * scale
            if top_k < s:
                vals, idx = jax.lax.top_k(scores, top_k)
                b_ix = jnp.arange(b)[:, None, None]
                t_ix = jnp.arange(t)[None, :, None]
                masked = jnp.full_like(scores, -jnp.inf)
                scores = masked.at[b_ix, t_ix, idx].set(vals)
            attn = jax.nn.softmax(scores, axis=-1)
            ctx = jnp.einsum('bts,bsd->btd', attn, v)
            return ctx @ Wo.T + bo
        return _read(query, mem_state, top_k, Wq, bq, Wk, bk, Wv, bv, Wo, bo)

    def _L0_ffn_ref(hidden_states, W1, b1, W2, b2):
        import jax, jax.numpy as jnp
        import numpy as np
        HIDDEN = 256
        INTER = 1024
        h = jax.nn.relu(jnp.einsum('bsh,hi->bsi', hidden_states, W1) + b1)
        return jnp.einsum('bsi,ih->bsh', h, W2) + b2
    x = x + jnp.tanh(g_xattn[0]) * _L0_xattn_ref(_layernorm(x, axis=-1), ctx_1024, 32, L0_xattn_Wq, L0_xattn_bq, L0_xattn_Wk, L0_xattn_bk, L0_xattn_Wv, L0_xattn_bv, L0_xattn_Wo, L0_xattn_bo)
    x = x + jnp.tanh(g_ffn[0]) * _L0_ffn_ref(_layernorm(x, axis=-1), L0_ffn_W1, L0_ffn_b1, L0_ffn_W2, L0_ffn_b2)
    return x

_drawn_inputs = setup_inputs


def setup_inputs(seed=0):
    import zlib

    import numpy as np

    out = dict(_drawn_inputs(seed))
    spreads = {'L0_xattn_bq': (0.0, 0.727),
     'L0_xattn_bk': (0.0, 0.8),
     'L0_xattn_bv': (0.0, 0.306),
     'L0_xattn_bo': (0.0, 0.1)}
    factors = {'L0_ffn_b1': 5.14, 'L0_ffn_b2': 3.7}
    for name, (base, spread) in spreads.items():
        noise = np.random.default_rng([zlib.crc32(name.encode()), seed]).standard_normal(out[name].shape)
        drawn = base * np.exp(spread * noise) if base else spread * noise
        out[name] = jnp.asarray(drawn.astype(out[name].dtype))
    for name, factor in factors.items():
        out[name] = (out[name] * factor).astype(out[name].dtype)
    return out
```

```python
import concourse.bass as bass
from concourse import mybir
from contextlib import ExitStack

B, T, S, D, F = 4, 1024, 154, 256, 1024
P = 128
TILES = 4
GROUP = TILES * P
GROUPS = B * T // GROUP
PER_BATCH = T // GROUP
KD = D // P
KF = F // P
SR = S - P
TOPK = 32
ROUNDS = TOPK // 8
STEPS = 4 * ROUNDS + 1
SCALE = float(D) ** -0.5
EPS = 1e-5
TAKEN = -3.4e38
HALF = B * S // 2


def gated_block(nc, x, w_qk, ctx_t, w_vo, small, w1, w2, out):
    f32, f32r = mybir.dt.float32, mybir.dt.float32r
    ALU, ACT = mybir.AluOpType, mybir.ActivationFunctionType

    stack = ExitStack()
    with stack:
        def sb(name, shape, dt=f32):
            return stack.enter_context(nc.sbuf_tensor(name, shape, dt))

        def bank(name):
            return stack.enter_context(nc.psum_tensor(name, [P, 512], f32))

        def sem(name):
            return stack.enter_context(nc.semaphore(name))

        with ExitStack() as early:
            def sb_early(name, shape, dt=f32):
                return early.enter_context(nc.sbuf_tensor(name, shape, dt))

            wqk_in = sb_early("wqk_in", [P, KD, 2 * D + 2])
            ctx_in = sb_early("ctx_in", [P, KD, B * S])
            wvo_in = sb_early("wvo_in", [P, KD, 2 * D + 1])
            bq_wide = sb_early("bq_wide", [P, KD, P])
            bv_wide = sb_early("bv_wide", [P, KD, P])
            wkq = sb_early("wkq", [P, KD, D + 1])
            kbq_wide = sb_early("kbq_wide", [P, KD, P])
            ctx_rest = sb_early("ctx_rest", [P, KD, B, P])
            w1_in = sb_early("w1_in", [P, KD, F])
            w2_in = sb_early("w2_in", [P, KF, D])

        x2b = sb("x2b", [P, TILES, D])
        hid = sb("hid", [P, 2, GROUP])
        hid_hi = sb("hid_hi", [P, KF, GROUP], f32r)
        hid_lo = sb("hid_lo", [P, KF, GROUP], f32r)
        x_all = sb("x_all", [P, GROUPS, TILES * D])
        small_in = sb("small_in", [P, 2 + KF + 2 * D])
        wk, wq = wqk_in[:, :, 0:D], wqk_in[:, :, D:2 * D]
        bq, bk = wqk_in[:, :, 2 * D:2 * D + 1], wqk_in[:, :, 2 * D + 1:2 * D + 2]
        wv, wo_t, bv = wvo_in[:, :, 0:D], wvo_in[:, :, D:2 * D], wvo_in[:, :, 2 * D:2 * D + 1]
        b1 = small_in[:, 2:2 + KF]
        bo = small_in[:, 2 + KF:2 + KF + D]
        b2 = small_in[:, 2 + KF + D:2 + KF + 2 * D]

        ident = sb("ident", [P, P])
        ones = sb("ones", [P, P])
        ones_r = sb("ones_r", [P, P], f32r)
        row0 = sb("row0", [P, P])
        neg_half = sb("neg_half", [P, TILES])

        tanh_g = sb("tanh_g", [P, 2])
        key_bias = sb("key_bias", [P, KD + 1])
        keys_hi = sb("keys_hi", [P, KD, B * S], f32r)
        keys_lo = sb("keys_lo", [P, KD, B * S], f32r)
        sbias_hi = sb("sbias_hi", [P, B * S], f32r)
        sbias = sb("sbias", [P, B * S], f32r)
        wvo = sb("wvo", [P, KD, D])
        vo_bias = sb("vo_bias", [P, D])
        values = sb("values", [P, 2, 2, D])
        vals_hi = sb("vals_hi", [P, B, D], f32r)
        vals_lo = sb("vals_lo", [P, B, D], f32r)
        vals_rest = sb("vals_rest", [P, B, D], f32r)
        w1_hi = sb("w1_hi", [P, KD, F], f32r)
        w1_lo = sb("w1_lo", [P, KD, F], f32r)
        w2_hi = sb("w2_hi", [P, KF, D], f32r)
        w2_lo = sb("w2_lo", [P, KF, D], f32r)
        b2_pair = sb("b2_pair", [P, 2, D])

        stats1 = sb("stats1", [P, TILES, 6])
        mv1 = sb("mv1", [P, TILES, 2])
        norm1 = sb("norm1", [P, 4, TILES])
        xn = sb("xn", [P, TILES, D])
        xnt_hi = sb("xnt_hi", [P, KD, GROUP], f32r)
        xnt_lo = sb("xnt_lo", [P, KD, GROUP], f32r)
        top = sb("top", [P, TILES, TOPK])
        neg_max = sb("neg_max", [P, TILES])
        left = sb("left", [P, TILES, S])
        probs = sb("probs", [P, TILES, S])
        picked = sb("picked", [P, TILES, 2 * P])
        denom = sb("denom", [P, TILES])
        inv_denom = sb("inv_denom", [P, TILES])
        pt_hi = sb("pt_hi", [P, 2, 2 * P], f32r)
        pt_lo = sb("pt_lo", [P, 2 * P], f32r)
        x2 = sb("x2", [P, TILES, D])
        stats2 = sb("stats2", [P, TILES, 6])
        mv2 = sb("mv2", [P, TILES, 2])
        norm2 = sb("norm2", [P, 3, TILES])
        x2n = sb("x2n", [P, TILES, D])
        x2nt_hi = sb("x2nt_hi", [P, KD, GROUP], f32r)
        x2nt_lo = sb("x2nt_lo", [P, KD, GROUP], f32r)
        y = sb("y", [P, TILES, D])

        z_ps = [bank("z_ps0"), bank("z_ps1")]
        tr_ps = [bank("tr_ps0"), bank("tr_ps1")]
        sc_ps = [bank("sc_ps0"), bank("sc_ps1")]
        y_ps = [bank("y_ps0"), bank("y_ps1")]

        qk_loaded, ctx_loaded, vo_loaded, small_loaded = sem("qk_loaded"), sem("ctx_loaded"), sem("vo_loaded"), sem("small_loaded")
        w1_loaded, w2_loaded, x_loaded = sem("w1_loaded"), sem("w2_loaded"), sem("x_loaded")
        vector_zeroed, pool_zeroed = sem("vector_zeroed"), sem("pool_zeroed")
        consts_made = sem("consts_made")
        tanh_made = sem("tanh_made")
        wide_made = sem("wide_made")
        wkq_ps_made, wkq_made, kbq_made = sem("wkq_ps_made"), sem("wkq_made"), sem("kbq_made")
        bias_ps_made, bias_made = sem("bias_ps_made"), sem("bias_made")
        keys_ps_made, keys_hi_made, keys_lo_made = sem("keys_ps_made"), sem("keys_hi_made"), sem("keys_lo_made")
        sbias_ps_made, sbias_hi_made, sbias_made = sem("sbias_ps_made"), sem("sbias_hi_made"), sem("sbias_made")
        rest_made = sem("rest_made")
        wvo_ps_made, wvo_made = sem("wvo_ps_made"), sem("wvo_made")
        vals_ps_made, vals_read, vals_lo_made = sem("vals_ps_made"), sem("vals_read"), sem("vals_lo_made")
        w1_hi_made, w2_hi_made, ffn_lo_made, b2_made = sem("w1_hi_made"), sem("w2_hi_made"), sem("ffn_lo_made"), sem("b2_made")
        stats1_step, norm1_step, xn_made = sem("stats1_step"), sem("norm1_step"), sem("xn_made")
        xnt_ps_made, xnt_hi_made, xnt_lo_made = sem("xnt_ps_made"), sem("xnt_hi_made"), sem("xnt_lo_made")
        scores_made, topk_step, probs_made = sem("scores_made"), sem("topk_step"), sem("probs_made")
        picked_made, rest_copied, inv_made = sem("picked_made"), sem("rest_copied"), sem("inv_made")
        pt_ps_made, pt_hi_made, pt_lo_made, att_made = sem("pt_ps_made"), sem("pt_hi_made"), sem("pt_lo_made"), sem("att_made")
        x2_made, stats2_step, norm2_step, x2n_made = sem("x2_made"), sem("stats2_step"), sem("norm2_step"), sem("x2n_made")
        x2nt_ps_made, x2nt_hi_made, x2nt_lo_made = sem("x2nt_ps_made"), sem("x2nt_hi_made"), sem("x2nt_lo_made")
        z_made, hid_made, hid_hi_made, hid_lo_made = sem("z_made"), sem("hid_made"), sem("hid_hi_made"), sem("hid_lo_made")
        x2b_made, ffn_made, y_made, y_stored = sem("x2b_made"), sem("ffn_made"), sem("y_made"), sem("y_stored")
        vector_waited, scalar_waited, pool_waited = sem("vector_waited"), sem("scalar_waited"), sem("pool_waited")

        def above_zero(count):
            return not isinstance(count, int) or count > 0

        def apart(eng, waited, index):
            if not isinstance(index, int):
                eng.sem_inc(waited, 1)

        def sweep(eng, turn):
            turn(None, None, 0)
            turn(0, None, 1)
            turn(1, 0, 2)
            with eng.Fori(2, GROUPS - 1) as i:
                turn(i, i - 1, i + 1)
            turn(GROUPS - 1, GROUPS - 2, None)
            turn(None, GROUPS - 1, None)

        block = stack.enter_context(nc.Block())

        @block.sync
        def _(sp):
            sp.dma_start(wqk_in[:], w_qk).then_inc(qk_loaded, 16)
            sp.dma_start(x_all[:, 0, :], x[0]).then_inc(x_loaded, 16)
            sp.dma_start(wvo_in[:], w_vo).then_inc(vo_loaded, 16)
            sp.wait_ge(x_loaded, 16)
            sp.dma_start(x_all[:, 1, :], x[1]).then_inc(x_loaded, 16)
            sp.dma_start(w1_in[:], w1).then_inc(w1_loaded, 16)
            sp.dma_start(w2_in[:], w2).then_inc(w2_loaded, 16)
            with sp.Fori(2, GROUPS) as i:
                sp.wait_ge(x_loaded, 16 * i)
                sp.dma_start(x_all[:, bass.ds(i, 1), :], x[bass.ds(i, 1)].rearrange("a p n -> p a n")).then_inc(x_loaded, 16)
            with sp.Fori(0, GROUPS) as i:
                sp.wait_ge(y_made, 2 * i + 2)
                sp.dma_start(out[bass.ds(i, 1)].rearrange("a p n -> p a n"),
                             y[:].rearrange("p j d -> p (j d)").unsqueeze(1)).then_inc(y_stored, 16)
            sp.wait_ge(y_stored, 16 * GROUPS)

        @block.tensor
        def _(pe):
            mm = pe.matmul

            def fold_keys():
                pe.wait_ge(qk_loaded, 16)
                for m in range(KD):
                    for k in range(KD):
                        last = mm(z_ps[m][:, 0:D + 1], wk[:, k, m * P:(m + 1) * P], wqk_in[:, k, D:2 * D + 1],
                                  start=k == 0, stop=k == KD - 1)
                    last.then_inc(wkq_ps_made, 1)
                for m in range(KD):
                    for k in range(KD):
                        mm(y_ps[0][:, m:m + 1], wq[:, k, m * P:(m + 1) * P], bk[:, k, :], start=k == 0, stop=k == KD - 1)
                pe.wait_ge(wide_made, 1)
                for k in range(KD):
                    last = mm(y_ps[0][:, KD:KD + 1], bq_wide[:, k, :], bk[:, k, :], start=k == 0, stop=k == KD - 1)
                last.then_inc(bias_ps_made, 1)
                pe.wait_ge(ctx_loaded, 16)
                for m in range(KD):
                    for h in range(2):
                        dst = (sc_ps, tr_ps)[h][m]
                        for k in range(KD):
                            pe.wait_ge(wkq_made, k + 1)
                            last = mm(dst[:, 0:HALF], wkq[:, k, m * P:(m + 1) * P], ctx_in[:, k, h * HALF:(h + 1) * HALF],
                                      start=k == 0, stop=k == KD - 1)
                        last.then_inc(keys_ps_made, 1)
                pe.wait_ge(kbq_made, 2)
                for h in range(2):
                    for k in range(KD):
                        last = mm(z_ps[h][:, 0:HALF], kbq_wide[:, k, :], ctx_in[:, k, h * HALF:(h + 1) * HALF],
                                  start=k == 0, stop=k == KD - 1)
                    last.then_inc(sbias_ps_made, 1)

            def fold_values():
                pe.wait_ge(vo_loaded, 16)
                pe.wait_ge(sbias_made, 4)
                for m in range(KD):
                    for k in range(KD):
                        last = mm(z_ps[m][:, 0:D], wv[:, k, m * P:(m + 1) * P], wo_t[:, k, :], start=k == 0, stop=k == KD - 1)
                    last.then_inc(wvo_ps_made, 1)
                pe.wait_ge(wide_made, 2)
                pe.wait_ge(small_loaded, 16)
                pe.wait_ge(bias_made, 1)
                for k in range(KD):
                    mm(y_ps[0][:, 0:D], bv_wide[:, k, :], wo_t[:, k, :], start=k == 0, stop=False)
                mm(y_ps[0][:, 0:D], row0[:], bo, start=False, stop=True).then_inc(wvo_ps_made, 1)
                pe.wait_ge(rest_made, 3)
                pe.wait_ge(wvo_made, 3)
                for n in range(2 * B):
                    b = n // 2
                    if above_zero(2 * (n - 1)):
                        pe.wait_ge(vals_read, 2 * (n - 1))
                    dst = z_ps[n % 2][:, 0:D]
                    for k in range(KD):
                        rows = ctx_rest[:, k, b, :] if n % 2 else ctx_in[:, k, b * S:b * S + P]
                        mm(dst, rows, wvo[:, k, :], start=k == 0, stop=False)
                    mm(dst, row0[:], vo_bias[:], start=False, stop=True).then_inc(vals_ps_made, 1)

            def transpose_xn(a, p):
                pe.wait_ge(xn_made, TILES * a + 2 * p + 2)
                if above_zero(2 * (a - 1) + p + 1):
                    pe.wait_ge(x2nt_lo_made, 2 * (a - 1) + p + 1)
                for k in range(KD):
                    for t in range(2):
                        last = pe.transpose(tr_ps[p][:, (2 * k + t) * P:(2 * k + t + 1) * P],
                                            xn[:, 2 * p + t, k * P:(k + 1) * P], ident[:])
                last.then_inc(xnt_ps_made, 1)

            def scores(a, j):
                pe.wait_ge(xnt_lo_made, 2 * a + j // 2 + 1)
                if above_zero(TILES * a + j - 1):
                    pe.wait_ge(probs_made, TILES * a + j - 1)
                at = (a // PER_BATCH) * S
                rows = slice(j * P, (j + 1) * P)
                dst = sc_ps[j % 2][:, 0:S]
                mm(dst, ones_r[:], sbias[:, bass.ds(at, S)], start=True, stop=False)
                for k in range(KD):
                    mm(dst, xnt_hi[:, k, rows], keys_hi[:, k, bass.ds(at, S)], start=False, stop=False)
                    mm(dst, xnt_hi[:, k, rows], keys_lo[:, k, bass.ds(at, S)], start=False, stop=False)
                    last = mm(dst, xnt_lo[:, k, rows], keys_hi[:, k, bass.ds(at, S)], start=False, stop=k == KD - 1)
                last.then_inc(scores_made, 1)

            def transpose_picked(a, p):
                pe.wait_ge(rest_copied, 2 * a + p + 1)
                pe.wait_ge(xnt_lo_made, 2 * a + p + 1)
                for c in range(2):
                    for t in range(2):
                        last = pe.transpose(tr_ps[p][:, (2 * c + t) * P:(2 * c + t + 1) * P],
                                            picked[:, 2 * p + t, c * P:(c + 1) * P], ident[:])
                last.then_inc(pt_ps_made, 1)

            def attend(a, p):
                pe.wait_ge(pt_lo_made, 4 * a + 2 * p + 2)
                if p == 0:
                    if above_zero(2 * (a - 1)):
                        pe.wait_ge(y_made, 2 * (a - 1))
                else:
                    pe.wait_ge(x2_made, TILES * a + 2)
                b = a // PER_BATCH
                for t in range(2):
                    dst = y_ps[0][:, t * D:(t + 1) * D]
                    rows = slice(t * P, (t + 1) * P)
                    hi, lo, rest = (v[:, bass.ds(b, 1), :].rearrange("p o d -> p (o d)") for v in (vals_hi, vals_lo, vals_rest))
                    mm(dst, pt_hi[:, 0, rows], hi, start=True, stop=False)
                    mm(dst, pt_hi[:, 0, rows], lo, start=False, stop=False)
                    mm(dst, pt_lo[:, rows], hi, start=False, stop=False)
                    last = mm(dst, pt_hi[:, 1, rows], rest, start=False, stop=True)
                last.then_inc(att_made, 1)

            def transpose_x2n(a, p):
                pe.wait_ge(x2n_made, TILES * a + 2 * p + 2)
                pe.wait_ge(pt_lo_made, 4 * a + 2 * p + 2)
                for k in range(KD):
                    for t in range(2):
                        last = pe.transpose(tr_ps[p][:, (2 * k + t) * P:(2 * k + t + 1) * P],
                                            x2n[:, 2 * p + t, k * P:(k + 1) * P], ident[:])
                last.then_inc(x2nt_ps_made, 1)

            def ffn_in(g, c):
                if c == 0:
                    pe.wait_ge(x2nt_lo_made, 2 * g + 2)
                if above_zero(KF * g + c - 1):
                    pe.wait_ge(hid_hi_made, KF * g + c - 1)
                dst = z_ps[c % 2]
                cols = slice(c * P, (c + 1) * P)
                for k in range(KD):
                    mm(dst[:], w1_hi[:, k, cols], x2nt_hi[:, k, :], start=k == 0, stop=False)
                    mm(dst[:], w1_hi[:, k, cols], x2nt_lo[:, k, :], start=False, stop=False)
                    last = mm(dst[:], w1_lo[:, k, cols], x2nt_hi[:, k, :], start=False, stop=k == KD - 1)
                last.then_inc(z_made, 1)

            def ffn_out(a, g, j):
                dst = y_ps[1 - j // 2][:, (j % 2) * D:(j % 2 + 1) * D]
                rows = slice(j * P, (j + 1) * P)
                if j == 0:
                    if above_zero(2 * g - 1):
                        pe.wait_ge(y_made, 2 * g - 1)
                    pe.wait_ge(hid_hi_made, KF * (g + 1))
                if j == 2:
                    pe.wait_ge(x2_made, TILES * (g + 1 if a is None else a + 1))
                    if above_zero(2 * g):
                        pe.wait_ge(y_made, 2 * g)
                for c in range(KF):
                    mm(dst, hid_hi[:, c, rows], w2_hi[:, c, :], start=c == 0, stop=False)
                    mm(dst, hid_hi[:, c, rows], w2_lo[:, c, :], start=False, stop=False)
                if j == 0:
                    pe.wait_ge(hid_lo_made, KF * (g + 1))
                for c in range(KF):
                    last = mm(dst, hid_lo[:, c, rows], w2_hi[:, c, :], start=False, stop=c == KF - 1)
                if j % 2:
                    last.then_inc(ffn_made, 1)

            def turn(a, g, n):
                if a is not None:
                    transpose_xn(a, 0)
                    transpose_xn(a, 1)
                if g is not None:
                    if isinstance(g, int):
                        pass
                    ffn_in(g, 0)
                if a is not None:
                    scores(a, 0)
                    scores(a, 1)
                if g is not None:
                    ffn_in(g, 1)
                    ffn_in(g, 2)
                if a is not None:
                    scores(a, 2)
                    scores(a, 3)
                    if g is None:
                        fold_values()
                if g is not None:
                    ffn_in(g, 3)
                    ffn_in(g, 4)
                if a is not None:
                    transpose_picked(a, 0)
                if g is not None:
                    ffn_in(g, 5)
                    ffn_in(g, 6)
                if a is not None:
                    if g is None:
                        pe.wait_ge(vals_lo_made, 2 * B)
                    attend(a, 0)
                if g is not None:
                    ffn_in(g, 7)
                if a is not None:
                    transpose_picked(a, 1)
                if g is not None:
                    ffn_out(a, g, 0)
                if a is not None:
                    attend(a, 1)
                if g is not None:
                    ffn_out(a, g, 1)
                if a is not None:
                    transpose_x2n(a, 0)
                if g is not None:
                    ffn_out(a, g, 2)
                    ffn_out(a, g, 3)
                if a is not None:
                    transpose_x2n(a, 1)
                    if g is None:
                        pe.wait_ge(ffn_lo_made, 2)

            fold_keys()
            pe.wait_ge(consts_made, 2)
            pe.wait_ge(sbias_made, 4)
            pe.wait_ge(keys_lo_made, 4)
            sweep(pe, turn)

        @block.scalar
        def _(act):
            func = act.activation
            act.dma_start(small_in[:], small).then_inc(small_loaded, 16)
            act.dma_start(ctx_in[:], ctx_t).then_inc(ctx_loaded, 16)

            def fold_keys():
                act.wait_ge(small_loaded, 16)
                func(tanh_g[:], small_in[:, 0:2], ACT.Tanh).then_inc(tanh_made, 1)
                act.wait_ge(bias_made, 1)
                for m in range(KD):
                    for h in range(2):
                        act.wait_ge(keys_ps_made, 2 * m + h + 1)
                        func(keys_hi[:, m, h * HALF:(h + 1) * HALF], (sc_ps, tr_ps)[h][m][:, 0:HALF], ACT.Identity,
                             bias=key_bias[:, m:m + 1]).then_inc(keys_hi_made, 1)
                for h in range(2):
                    act.wait_ge(sbias_ps_made, h + 1)
                    func(sbias_hi[:, h * HALF:(h + 1) * HALF], z_ps[h][:, 0:HALF], ACT.Identity,
                         bias=key_bias[:, KD:KD + 1]).then_inc(sbias_hi_made, 1)

            def fold_wvo():
                act.wait_ge(tanh_made, 1)
                for m in range(KD):
                    act.wait_ge(wvo_ps_made, m + 1)
                    func(wvo[:, m, :], z_ps[m][:, 0:D], ACT.Identity, scale=tanh_g[:, 0:1]).then_inc(wvo_made, 1)
                act.wait_ge(wvo_ps_made, 3)
                func(vo_bias[:], y_ps[0][:, 0:D], ACT.Identity, scale=tanh_g[:, 0:1]).then_inc(wvo_made, 1)

            def split_values(n):
                b = n // 2
                act.wait_ge(vals_ps_made, n + 1)
                if above_zero(n - 3):
                    act.wait_ge(vals_lo_made, n - 3)
                func(values[:, n % 2, b % 2, :], z_ps[n % 2][:, 0:D], ACT.Copy).then_inc(vals_read, 1)
                hi = vals_rest if n % 2 else vals_hi
                func(hi[:, b, :], z_ps[n % 2][:, 0:D], ACT.Copy).then_inc(vals_read, 1)

            def split_ffn_weights():
                act.wait_ge(w1_loaded, 16)
                func(w1_hi[:], w1_in[:], ACT.Copy).then_inc(w1_hi_made, 1)
                act.wait_ge(w2_loaded, 16)
                func(w2_hi[:], w2_in[:], ACT.Identity, scale=tanh_g[:, 1:2]).then_inc(w2_hi_made, 1)
                func(w2_in[:], w2_in[:], ACT.Identity, scale=tanh_g[:, 1:2]).then_inc(w2_hi_made, 1)

            def normalise_x(n):
                act.wait_ge(norm1_step, 4 * (n + 1))
                if above_zero(2 * n):
                    act.wait_ge(xnt_ps_made, 2 * n)
                apart(act, scalar_waited, n)
                for j in range(TILES):
                    rows = x_all[:, bass.ds(n, 1), j * D:(j + 1) * D].rearrange("p o d -> p (o d)")
                    func(xn[:, j, :], rows, ACT.Identity, scale=norm1[:, 2, j:j + 1],
                         bias=norm1[:, 3, j:j + 1]).then_inc(xn_made, 1)

            def xnt_to_hi(a, p):
                act.wait_ge(xnt_ps_made, 2 * a + p + 1)
                func(xnt_hi[:, :, 2 * p * P:2 * (p + 1) * P], tr_ps[p][:].rearrange("p (k c) -> p k c", k=KD),
                     ACT.Copy).then_inc(xnt_hi_made, 1)

            def exps(a, p):
                for t in range(2):
                    j = 2 * p + t
                    act.wait_ge(topk_step, (2 * a + p) * STEPS + 4 + t)
                    func(probs[:, j, :], sc_ps[t][:, 0:S], ACT.Exp, bias=neg_max[:, j:j + 1], scale=SCALE).then_inc(probs_made, 1)

            def copy_rest(a, p):
                act.wait_ge(picked_made, TILES * a + 2 * p + 2)
                rest = picked[:, 2 * p:2 * p + 2, P:2 * P].rearrange("p j (r c) -> p j r c", c=32)
                func(rest[:, :, 1:3, 0:SR], rest[:, :, 0:1, 0:SR].to_broadcast([P, 2, 2, SR]), ACT.Copy).then_inc(rest_copied, 1)

            def pt_to_hi(a, p):
                act.wait_ge(pt_ps_made, 2 * a + p + 1)
                if above_zero(2 * a + p):
                    act.wait_ge(att_made, 2 * a + p)
                func(pt_hi[:], tr_ps[p][:].rearrange("p (k c) -> p k c", k=2), ACT.Copy).then_inc(pt_hi_made, 1)

            def x2nt_to_hi(a, p):
                act.wait_ge(x2nt_ps_made, 2 * a + p + 1)
                func(x2nt_hi[:, :, 2 * p * P:2 * (p + 1) * P], tr_ps[p][:].rearrange("p (k c) -> p k c", k=KD),
                     ACT.Copy).then_inc(x2nt_hi_made, 1)

            def relu(g, c):
                act.wait_ge(z_made, KF * g + c + 1)
                if above_zero(KF * g + c - 1):
                    act.wait_ge(hid_lo_made, KF * g + c - 1)
                func(hid[:, c % 2, :], z_ps[c % 2][:], ACT.Relu, bias=b1[:, c:c + 1]).then_inc(hid_made, 1)
                func(hid_hi[:, c, :], z_ps[c % 2][:], ACT.Relu, bias=b1[:, c:c + 1]).then_inc(hid_hi_made, 1)

            def turn(a, g, n):
                if a is not None:
                    xnt_to_hi(a, 0)
                    xnt_to_hi(a, 1)
                if g is not None:
                    relu(g, 0)
                if a is not None:
                    exps(a, 0)
                    if g is None:
                        fold_wvo()
                        split_values(0)
                        split_values(1)
                if g is not None:
                    relu(g, 1)
                    relu(g, 2)
                    relu(g, 3)
                if a is not None:
                    copy_rest(a, 0)
                    exps(a, 1)
                    if g is None:
                        for n_out in range(2, 2 * B):
                            split_values(n_out)
                if g is not None:
                    relu(g, 4)
                if a is not None:
                    pt_to_hi(a, 0)
                if g is not None:
                    relu(g, 5)
                    relu(g, 6)
                    relu(g, 7)
                if a is not None:
                    copy_rest(a, 1)
                    if g is None:
                        split_ffn_weights()
                    pt_to_hi(a, 1)
                if n is not None:
                    normalise_x(n)
                if a is not None:
                    x2nt_to_hi(a, 0)
                    x2nt_to_hi(a, 1)

            fold_keys()
            sweep(act, turn)

        @block.vector
        def _(dve):
            def fold_keys():
                nc.vector.memset(ones[:], 1.0).then_inc(vector_zeroed, 1)
                nc.vector.memset(sbias[:].bitcast(f32), 0.0).then_inc(vector_zeroed, 1)
                nc.vector.memset(picked[:], 0.0).then_inc(vector_zeroed, 1)
                dve.wait_ge(vector_zeroed, 3)
                nc.vector.tensor_copy(ones_r[:], ones[:])
                dve.wait_ge(qk_loaded, 16)
                for k in range(KD):
                    last = nc.vector.tensor_scalar(bq_wide[:, k, :], ones[:], bq[:, k, :], None, ALU.mult)
                last.then_inc(wide_made, 1)
                for m in range(KD):
                    dve.wait_ge(wkq_ps_made, m + 1)
                    nc.vector.tensor_copy(wkq[:, m, :], z_ps[m][:, 0:D + 1]).then_inc(wkq_made, 1)
                for m in range(KD):
                    dve.wait_ge(wkq_made, m + 1)
                    nc.vector.tensor_scalar(kbq_wide[:, m, :], ones[:], wkq[:, m, D:D + 1], None, ALU.mult).then_inc(kbq_made, 1)
                dve.wait_ge(bias_ps_made, 1)
                nc.vector.tensor_copy(key_bias[:], y_ps[0][:, 0:KD + 1]).then_inc(bias_made, 1)
                dve.wait_ge(bias_made, 1)
                for m in range(KD):
                    for h in range(2):
                        dve.wait_ge(keys_hi_made, 2 * m + h + 1)
                        cols = slice(h * HALF, (h + 1) * HALF)
                        nc.vector.scalar_tensor_tensor(keys_lo[:, m, cols], (sc_ps, tr_ps)[h][m][:, 0:HALF], key_bias[:, m:m + 1],
                                                       keys_hi[:, m, cols], ALU.add, ALU.subtract).then_inc(keys_lo_made, 1)
                for h in range(2):
                    cols = slice(h * HALF, (h + 1) * HALF)
                    dve.wait_ge(sbias_hi_made, h + 1)
                    nc.vector.tensor_copy(sbias[0:1, cols], sbias_hi[0:1, cols]).then_inc(sbias_made, 1)
                    nc.vector.scalar_tensor_tensor(sbias[32:33, cols], z_ps[h][32:33, 0:HALF], key_bias[32:33, KD:KD + 1],
                                                   sbias_hi[32:33, cols], ALU.add, ALU.subtract).then_inc(sbias_made, 1)
                dve.wait_ge(vo_loaded, 16)
                for k in range(KD):
                    last = nc.vector.tensor_scalar(bv_wide[:, k, :], ones[:], bv[:, k, :], None, ALU.mult)
                last.then_inc(wide_made, 1)

            def stats_x(n):
                dve.wait_ge(x_loaded, 16 * (n + 1))
                if above_zero(4 * n):
                    dve.wait_ge(norm1_step, 4 * n)
                apart(dve, vector_waited, n)
                for j in range(TILES):
                    rows = x_all[:, bass.ds(n, 1), j * D:(j + 1) * D].rearrange("p o d -> p (o d)")
                    nc.vector.bn_stats(stats1[:, j, :], rows).then_inc(stats1_step, 1)
                for j in range(TILES):
                    dve.wait_ge(stats1_step, 2 * TILES * n + j + 1)
                    apart(dve, vector_waited, n)
                    nc.vector.bn_aggr(mv1[:, j, :], stats1[:, j, :]).then_inc(stats1_step, 1)

            def xnt_to_lo(a, p):
                dve.wait_ge(xnt_hi_made, 2 * a + p + 1)
                cols = slice(2 * p * P, 2 * (p + 1) * P)
                nc.vector.tensor_tensor(xnt_lo[:, :, cols], tr_ps[p][:].rearrange("p (k c) -> p k c", k=KD),
                                        xnt_hi[:, :, cols], ALU.subtract).then_inc(xnt_lo_made, 1)

            def topk_round(a, p, r):
                done = (2 * a + p) * STEPS
                at = 0 if r == 0 else 4 * r + 1
                for t in range(2):
                    j = 2 * p + t
                    if r == 0:
                        dve.wait_ge(scores_made, TILES * a + j + 1)
                    else:
                        dve.wait_ge(topk_step, done + at - 1 + t)
                    apart(dve, vector_waited, a)
                    nc.vector.max(top[:, j, 8 * r:8 * r + 8], sc_ps[t][:, 0:S] if r == 0 else left[:, j, :]).then_inc(topk_step, 1)
                if r == 0:
                    dve.wait_ge(topk_step, done + 2)
                    nc.vector.tensor_scalar(neg_max[:, 2 * p:2 * p + 2], top[:, 2 * p:2 * p + 2, 0], -SCALE, None,
                                            ALU.mult).then_inc(topk_step, 1)
                for t in range(2):
                    j = 2 * p + t
                    dve.wait_ge(topk_step, done + at + 1 + t)
                    apart(dve, vector_waited, a)
                    nc.vector.match_replace(left[:, j, :], top[:, j, 8 * r:8 * r + 8], sc_ps[t][:, 0:S] if r == 0 else left[:, j, :],
                                            TAKEN).then_inc(topk_step, 1)

            def pick(a, p):
                for t in range(2):
                    j = 2 * p + t
                    dve.wait_ge(topk_step, (2 * a + p) * STEPS + STEPS - 1 + t)
                    dve.wait_ge(probs_made, TILES * a + j + 1)
                    nc.vector.scalar_tensor_tensor(picked[:, j, 0:S], left[:, j, :], TAKEN, probs[:, j, :], ALU.is_equal, ALU.mult,
                                                   accum_out=denom[:, j:j + 1]).then_inc(picked_made, 1)

            def invert(a, p):
                dve.wait_ge(picked_made, TILES * a + 2 * p + 2)
                nc.vector.reciprocal(inv_denom[:, 2 * p:2 * p + 2], denom[:, 2 * p:2 * p + 2]).then_inc(inv_made, 1)

            def pt_to_lo(a, p):
                dve.wait_ge(pt_hi_made, 2 * a + p + 1)
                nc.vector.tensor_tensor(pt_lo[:], tr_ps[p][:, 0:2 * P], pt_hi[:, 0, :], ALU.subtract).then_inc(pt_lo_made, 1)
                nc.vector.tensor_tensor(pt_hi[32:64, 1, :], tr_ps[p][32:64, 2 * P:4 * P], pt_hi[32:64, 1, :],
                                        ALU.subtract).then_inc(pt_lo_made, 1)

            def residual(a, p):
                dve.wait_ge(att_made, 2 * a + p + 1)
                dve.wait_ge(inv_made, 2 * a + p + 1)
                if above_zero(2 * (a - 1) + p + 1):
                    dve.wait_ge(x2b_made, 2 * (a - 1) + p + 1)
                apart(dve, vector_waited, a)
                for t in range(2):
                    j = 2 * p + t
                    rows = x_all[:, bass.ds(a, 1), j * D:(j + 1) * D].rearrange("p o d -> p (o d)")
                    nc.vector.scalar_tensor_tensor(x2[:, j, :], y_ps[0][:, t * D:(t + 1) * D], inv_denom[:, j:j + 1], rows,
                                                   ALU.mult, ALU.add).then_inc(x2_made, 1)
                for t in range(2):
                    j = 2 * p + t
                    dve.wait_ge(x2_made, TILES * a + j + 1)
                    nc.vector.bn_stats(stats2[:, j, :], x2[:, j, :]).then_inc(stats2_step, 1)
                for t in range(2):
                    j = 2 * p + t
                    dve.wait_ge(stats2_step, 2 * TILES * a + 4 * p + t + 1)
                    apart(dve, vector_waited, a)
                    nc.vector.bn_aggr(mv2[:, j, :], stats2[:, j, :]).then_inc(stats2_step, 1)

            def x2nt_to_lo(a, p):
                dve.wait_ge(x2nt_hi_made, 2 * a + p + 1)
                cols = slice(2 * p * P, 2 * (p + 1) * P)
                nc.vector.tensor_tensor(x2nt_lo[:, :, cols], tr_ps[p][:].rearrange("p (k c) -> p k c", k=KD),
                                        x2nt_hi[:, :, cols], ALU.subtract).then_inc(x2nt_lo_made, 1)

            def output(g, p):
                dve.wait_ge(ffn_made, 2 * g + p + 1)
                dve.wait_ge(x2b_made, 2 * g + 2)
                if above_zero(16 * g):
                    dve.wait_ge(y_stored, 16 * g)
                nc.vector.tensor_tensor(y[:, 2 * p:2 * p + 2, :], y_ps[1 - p][:].rearrange("p (j d) -> p j d", j=2),
                                        x2b[:, 2 * p:2 * p + 2, :], ALU.add).then_inc(y_made, 1)

            def turn(a, g, n):
                if a is not None:
                    xnt_to_lo(a, 0)
                    xnt_to_lo(a, 1)
                    for r in range(ROUNDS):
                        topk_round(a, 0, r)
                    pick(a, 0)
                    invert(a, 0)
                    topk_round(a, 1, 0)
                    topk_round(a, 1, 1)
                    pt_to_lo(a, 0)
                    topk_round(a, 1, 2)
                    topk_round(a, 1, 3)
                    pick(a, 1)
                    invert(a, 1)
                    residual(a, 0)
                    pt_to_lo(a, 1)
                if n is not None:
                    stats_x(n)
                if a is not None and g is None:
                    residual(a, 1)
                    x2nt_to_lo(a, 0)
                    x2nt_to_lo(a, 1)
                elif a is not None:
                    residual(a, 1)
                    output(g, 0)
                    x2nt_to_lo(a, 0)
                    output(g, 1)
                    x2nt_to_lo(a, 1)
                elif g is not None:
                    output(g, 0)
                    output(g, 1)

            fold_keys()
            sweep(dve, turn)

        @block.gpsimd
        def _(pool):
            def prepare():
                nc.gpsimd.memset(ident[:], 0.0).then_inc(pool_zeroed, 1)
                nc.gpsimd.memset(row0[:], 0.0).then_inc(pool_zeroed, 1)
                nc.gpsimd.memset(ctx_rest[:], 0.0).then_inc(pool_zeroed, 1)
                nc.gpsimd.memset(neg_half[:], -0.5).then_inc(pool_zeroed, 1)
                pool.wait_ge(pool_zeroed, 4)
                nc.gpsimd.affine_select(out=ident[:], in_=ident[:], compare_op=ALU.not_equal, fill=1.0, base=0,
                                        pattern=[[-1, P]], channel_multiplier=1).then_inc(consts_made, 1)
                nc.gpsimd.memset(row0[0:1, :], 1.0).then_inc(consts_made, 1)
                pool.wait_ge(ctx_loaded, 16)
                by_batch = ctx_in[:].rearrange("p k (b s) -> p k b s", b=B)
                for r in range(3):
                    for k in range(KD):
                        last = nc.gpsimd.tensor_copy(ctx_rest[:, k, :, 32 * r:32 * r + SR], by_batch[:, k, :, P:S])
                    last.then_inc(rest_made, 1)

            def values_to_lo(n):
                pool.wait_ge(vals_read, 2 * n + 2)
                if above_zero(n):
                    pool.wait_ge(vals_lo_made, n)
                b = n // 2
                if n % 2:
                    nc.gpsimd.tensor_tensor(vals_rest[64:96, b, :], values[64:96, 1, b % 2, :], vals_rest[64:96, b, :],
                                            ALU.subtract).then_inc(vals_lo_made, 1)
                else:
                    nc.gpsimd.tensor_tensor(vals_lo[:, b, :], values[:, 0, b % 2, :], vals_hi[:, b, :],
                                            ALU.subtract).then_inc(vals_lo_made, 1)

            def split_ffn_weights():
                pool.wait_ge(tanh_made, 1)
                pool.wait_ge(vals_lo_made, 2 * B)
                nc.gpsimd.tensor_scalar(b2_pair[:, 0, :], b2, tanh_g[:, 1:2], None, ALU.mult).then_inc(b2_made, 1)
                nc.gpsimd.tensor_scalar(b2_pair[:, 1, :], b2, tanh_g[:, 1:2], None, ALU.mult).then_inc(b2_made, 1)
                pool.wait_ge(w1_hi_made, 1)
                nc.gpsimd.tensor_tensor(w1_lo[:], w1_in[:], w1_hi[:], ALU.subtract).then_inc(ffn_lo_made, 1)
                pool.wait_ge(w2_hi_made, 2)
                nc.gpsimd.tensor_tensor(w2_lo[:], w2_in[:], w2_hi[:], ALU.subtract).then_inc(ffn_lo_made, 1)

            def rstd_x(n):
                pool.wait_ge(stats1_step, 2 * TILES * (n + 1))
                if above_zero(TILES * n):
                    pool.wait_ge(xn_made, TILES * n)
                apart(pool, pool_waited, n)
                nc.gpsimd.tensor_scalar(norm1[:, 0, :], mv1[:, :, 1], EPS, 1.0, ALU.add, ALU.mult).then_inc(norm1_step, 1)
                nc.gpsimd.tensor_scalar(norm1[:, 1, :], mv1[:, :, 0], -1.0, 0.0, ALU.mult, ALU.add).then_inc(norm1_step, 1)
                pool.wait_ge(norm1_step, 4 * n + 1)
                nc.gpsimd.tensor_tensor(norm1[:, 2, :], norm1[:, 0, :], neg_half[:], ALU.pow).then_inc(norm1_step, 1)
                pool.wait_ge(norm1_step, 4 * n + 3)
                nc.gpsimd.tensor_tensor(norm1[:, 3, :], norm1[:, 1, :], norm1[:, 2, :], ALU.mult).then_inc(norm1_step, 1)

            def normalise_x2(a, p):
                cols = slice(2 * p, 2 * p + 2)
                pool.wait_ge(stats2_step, 2 * TILES * a + 4 * p + 4)
                apart(pool, pool_waited, a)
                nc.gpsimd.tensor_scalar(norm2[:, 0, cols], mv2[:, cols, 1], EPS, 1.0, ALU.add, ALU.mult).then_inc(norm2_step, 1)
                nc.gpsimd.tensor_scalar(norm2[:, 1, cols], mv2[:, cols, 0], -1.0, 0.0, ALU.mult, ALU.add).then_inc(norm2_step, 1)
                pool.wait_ge(norm2_step, 6 * a + 3 * p + 1)
                nc.gpsimd.tensor_tensor(norm2[:, 2, cols], norm2[:, 0, cols], neg_half[:, 0:2], ALU.pow).then_inc(norm2_step, 1)
                pool.wait_ge(norm2_step, 6 * a + 3 * p + 3)
                if above_zero(2 * (a - 1) + p + 1):
                    pool.wait_ge(x2nt_ps_made, 2 * (a - 1) + p + 1)
                apart(pool, pool_waited, a)
                for t in range(2):
                    j = 2 * p + t
                    nc.gpsimd.tensor_scalar(x2n[:, j, :], x2[:, j, :], norm2[:, 1, j:j + 1], norm2[:, 2, j:j + 1],
                                            ALU.add, ALU.mult).then_inc(x2n_made, 1)

            def add_b2(g):
                for p in range(2):
                    if above_zero(2 * (g - 1) + p + 1):
                        pool.wait_ge(y_made, 2 * (g - 1) + p + 1)
                    pool.wait_ge(x2_made, TILES * g + 2 * p + 2)
                    pair = slice(2 * p, 2 * p + 2)
                    nc.gpsimd.tensor_tensor(x2b[:, pair, :], x2[:, pair, :], b2_pair[:], ALU.add).then_inc(x2b_made, 1)

            def hid_to_lo(g, c):
                pool.wait_ge(hid_hi_made, KF * g + c + 1)
                pool.wait_ge(hid_made, KF * g + c + 1)
                if above_zero(2 * g):
                    pool.wait_ge(ffn_made, 2 * g)
                nc.gpsimd.tensor_tensor(hid_lo[:, c, :], hid[:, c % 2, :], hid_hi[:, c, :], ALU.subtract).then_inc(hid_lo_made, 1)

            def turn(a, g, n):
                if a is not None and g is None:
                    for n_out in range(2 * B):
                        values_to_lo(n_out)
                    split_ffn_weights()
                if g is not None:
                    add_b2(g)
                    for c in range(KF):
                        hid_to_lo(g, c)
                if n is not None and a is None:
                    rstd_x(n)
                if a is not None:
                    normalise_x2(a, 0)
                    if n is not None:
                        rstd_x(n)
                    normalise_x2(a, 1)

            prepare()
            sweep(pool, turn)


def kernel(x, ctx_1024, g_xattn, g_ffn, L0_xattn_Wq, L0_xattn_bq, L0_xattn_Wk, L0_xattn_bk, L0_xattn_Wv, L0_xattn_bv,
           L0_xattn_Wo, L0_xattn_bo, L0_ffn_W1, L0_ffn_b1, L0_ffn_W2, L0_ffn_b2):
    import numpy as np
    import concourse.bacc as bacc
    from concourse.bass_utils import run_bass_kernel_spmd

    def by_partition(a):
        a = np.asarray(a)
        return a.reshape(-1, P, a.shape[-1]).transpose(1, 0, 2)

    def column(v):
        return by_partition(np.asarray(v)[:, None])

    def everywhere(v):
        v = np.asarray(v)
        return np.broadcast_to(v, (P, v.size))

    ctx_rows = np.asarray(ctx_1024).reshape(B * S, D)
    arrays = {
        "x": np.asarray(x).reshape(GROUPS, P, TILES * D),
        "w_qk": np.concatenate([by_partition(L0_xattn_Wk), by_partition(L0_xattn_Wq), column(L0_xattn_bq), column(L0_xattn_bk)], axis=2),
        "ctx_t": by_partition(ctx_rows.T),
        "w_vo": np.concatenate([by_partition(L0_xattn_Wv), by_partition(np.asarray(L0_xattn_Wo).T), column(L0_xattn_bv)], axis=2),
        "small": np.concatenate([everywhere(g_xattn), everywhere(g_ffn), np.asarray(L0_ffn_b1).reshape(KF, P).T,
                                 everywhere(L0_xattn_bo), everywhere(L0_ffn_b2)], axis=1),
        "w1": by_partition(L0_ffn_W1),
        "w2": by_partition(L0_ffn_W2),
    }
    arrays = {k: np.ascontiguousarray(v) for k, v in arrays.items()}
    nc = bacc.Bacc("TRN2", target_bir_lowering=False, num_devices=1)
    args = [nc.dram_tensor(k, v.shape, mybir.dt.float32, kind="ExternalInput").ap() for k, v in arrays.items()]
    out = nc.dram_tensor("out", (GROUPS, P, TILES * D), mybir.dt.float32, kind="ExternalOutput").ap()
    gated_block(nc, *args, out)
    r = run_bass_kernel_spmd(nc, [arrays], core_ids=[0])
    return r.results[0]["out"].reshape(B, T, D)
```

```python
import concourse.bass as bass
from concourse import mybir
from contextlib import ExitStack

B, T, S, D, F = 4, 1024, 154, 256, 1024
P = 128
TILES = 4
GROUP = TILES * P
GROUPS = B * T // GROUP
PER_BATCH = T // GROUP
KD = D // P
KF = F // P
SR = S - P
TOPK = 32
ROUNDS = TOPK // 8
STEPS = 4 * ROUNDS + 1
SCALE = float(D) ** -0.5
EPS = 1e-5
TAKEN = -3.4e38
HALF = B * S // 2


def gated_block(nc, x, x_t, w_qk, ctx_t, w_vo, small, w1, w2, out):
    f32, f32r = mybir.dt.float32, mybir.dt.float32r
    ALU, ACT = mybir.AluOpType, mybir.ActivationFunctionType

    stack = ExitStack()
    with stack:
        def sb(name, shape, dt=f32):
            return stack.enter_context(nc.sbuf_tensor(name, shape, dt))

        def bank(name):
            return stack.enter_context(nc.psum_tensor(name, [P, 512], f32))

        def sem(name):
            return stack.enter_context(nc.semaphore(name))

        with ExitStack() as early:
            def sb_early(name, shape, dt=f32):
                return early.enter_context(nc.sbuf_tensor(name, shape, dt))

            wqk_in = sb_early("wqk_in", [P, KD, 2 * D + 2])
            ctx_in = sb_early("ctx_in", [P, KD, B * S])
            wvo_in = sb_early("wvo_in", [P, KD, 2 * D + 1])
            bq_wide = sb_early("bq_wide", [P, KD, P])
            bv_wide = sb_early("bv_wide", [P, KD, P])
            wkq = sb_early("wkq", [P, KD, D + 1])
            kbq_wide = sb_early("kbq_wide", [P, KD, P])
            ctx_rest = sb_early("ctx_rest", [P, KD, B, P])
            w1_in = sb_early("w1_in", [P, KD, F])
            w2_in = sb_early("w2_in", [P, KF, D])

        x2b = sb("x2b", [P, TILES, D])
        hid = sb("hid", [P, 2, GROUP])
        hid_hi = sb("hid_hi", [P, KF, GROUP], f32r)
        hid_lo = sb("hid_lo", [P, KF, GROUP], f32r)
        x_all = sb("x_all", [P, GROUPS, TILES * D])
        small_in = sb("small_in", [P, 2 + KF + 2 * D])
        wk, wq = wqk_in[:, :, 0:D], wqk_in[:, :, D:2 * D]
        bq, bk = wqk_in[:, :, 2 * D:2 * D + 1], wqk_in[:, :, 2 * D + 1:2 * D + 2]
        wv, wo_t, bv = wvo_in[:, :, 0:D], wvo_in[:, :, D:2 * D], wvo_in[:, :, 2 * D:2 * D + 1]
        b1 = small_in[:, 2:2 + KF]
        bo = small_in[:, 2 + KF:2 + KF + D]
        b2 = small_in[:, 2 + KF + D:2 + KF + 2 * D]

        ident = sb("ident", [P, P])
        ones = sb("ones", [P, P])
        row0 = sb("row0", [P, P])
        neg_half = sb("neg_half", [P, TILES])

        tanh_g = sb("tanh_g", [P, 2])
        key_bias = sb("key_bias", [P, KD + 1])
        keys_hi = sb("keys_hi", [P, KD, B * S], f32r)
        keys_lo = sb("keys_lo", [P, KD, B * S], f32r)
        score_bias = sb("score_bias", [P, B * S])
        wq_stats = sb("wq_stats", [P, KD, 6])
        wq_mean = sb("wq_mean", [P, KD, 2])
        wvo = sb("wvo", [P, KD, D])
        vo_bias = sb("vo_bias", [P, D])
        values = sb("values", [P, 2, 2, D])
        vals_hi = sb("vals_hi", [P, B, D], f32r)
        vals_lo = sb("vals_lo", [P, B, D], f32r)
        vals_rest = sb("vals_rest", [P, B, D], f32r)
        w1_hi = sb("w1_hi", [P, KD, F], f32r)
        w1_lo = sb("w1_lo", [P, KD, F], f32r)
        w2_hi = sb("w2_hi", [P, KF, D], f32r)
        w2_lo = sb("w2_lo", [P, KF, D], f32r)
        b2_pair = sb("b2_pair", [P, 2, D])

        stats1 = sb("stats1", [P, TILES, 6])
        mv1 = sb("mv1", [P, TILES, 2])
        norm1 = sb("norm1", [P, 2, TILES])
        xt_in = sb("xt_in", [P, KD, GROUP])
        xt_hi = sb("xt_hi", [P, KD, GROUP], f32r)
        xt_lo = sb("xt_lo", [P, KD, GROUP], f32r)
        score = sb("score", [P, TILES, S])
        top = sb("top", [P, TILES, TOPK])
        neg_max = sb("neg_max", [P, TILES])
        left = sb("left", [P, TILES, S])
        probs = sb("probs", [P, TILES, S])
        picked = sb("picked", [P, TILES, 2 * P])
        denom = sb("denom", [P, TILES])
        inv_denom = sb("inv_denom", [P, TILES])
        pt_hi = sb("pt_hi", [P, 2, 2 * P], f32r)
        pt_lo = sb("pt_lo", [P, 2 * P], f32r)
        x2 = sb("x2", [P, TILES, D])
        stats2 = sb("stats2", [P, TILES, 6])
        mv2 = sb("mv2", [P, TILES, 2])
        norm2 = sb("norm2", [P, 3, TILES])
        x2n = sb("x2n", [P, TILES, D])
        x2nt_hi = sb("x2nt_hi", [P, KD, GROUP], f32r)
        x2nt_lo = sb("x2nt_lo", [P, KD, GROUP], f32r)
        y = sb("y", [P, TILES, D])

        z_ps = [bank("z_ps0"), bank("z_ps1")]
        tr_ps = [bank("tr_ps0"), bank("tr_ps1")]
        sc_ps = [bank("sc_ps0"), bank("sc_ps1")]
        y_ps = [bank("y_ps0"), bank("y_ps1")]

        qk_loaded, ctx_loaded, vo_loaded, small_loaded = sem("qk_loaded"), sem("ctx_loaded"), sem("vo_loaded"), sem("small_loaded")
        w1_loaded, w2_loaded, x_loaded, xt_loaded = sem("w1_loaded"), sem("w2_loaded"), sem("x_loaded"), sem("xt_loaded")
        vector_zeroed, pool_zeroed = sem("vector_zeroed"), sem("pool_zeroed")
        consts_made = sem("consts_made")
        tanh_made = sem("tanh_made")
        wide_made = sem("wide_made")
        wkq_ps_made, wkq_made, kbq_made = sem("wkq_ps_made"), sem("wkq_made"), sem("kbq_made")
        bias_ps_made, bias_made = sem("bias_ps_made"), sem("bias_made")
        keys_ps_made, keys_hi_made, keys_lo_made = sem("keys_ps_made"), sem("keys_hi_made"), sem("keys_lo_made")
        wq_step, sbias_ps_made, sbias_made = sem("wq_step"), sem("sbias_ps_made"), sem("sbias_made")
        rest_made = sem("rest_made")
        wvo_ps_made, wvo_made = sem("wvo_ps_made"), sem("wvo_made")
        vals_ps_made, vals_read, vals_lo_made = sem("vals_ps_made"), sem("vals_read"), sem("vals_lo_made")
        w1_hi_made, w2_hi_made, b2_made = sem("w1_hi_made"), sem("w2_hi_made"), sem("b2_made")
        w1_lo_made, w2_lo_made = sem("w1_lo_made"), sem("w2_lo_made")
        stats1_step, norm1_step = sem("stats1_step"), sem("norm1_step")
        xt_hi_made, xt_lo_made = sem("xt_hi_made"), sem("xt_lo_made")
        scores_made, scaled_made, topk_step, probs_made = sem("scores_made"), sem("scaled_made"), sem("topk_step"), sem("probs_made")
        picked_made, rest_copied, inv_made = sem("picked_made"), sem("rest_copied"), sem("inv_made")
        pt_ps_made, pt_hi_made, pt_lo_made, att_made = sem("pt_ps_made"), sem("pt_hi_made"), sem("pt_lo_made"), sem("att_made")
        x2_made, stats2_step, norm2_step, x2n_made = sem("x2_made"), sem("stats2_step"), sem("norm2_step"), sem("x2n_made")
        x2nt_ps_made, x2nt_hi_made, x2nt_lo_made = sem("x2nt_ps_made"), sem("x2nt_hi_made"), sem("x2nt_lo_made")
        z_made, hid_made, hid_hi_made, hid_lo_made = sem("z_made"), sem("hid_made"), sem("hid_hi_made"), sem("hid_lo_made")
        x2b_made, ffn_made, y_made, y_stored = sem("x2b_made"), sem("ffn_made"), sem("y_made"), sem("y_stored")
        vector_waited, pool_waited = sem("vector_waited"), sem("pool_waited")

        def above_zero(count):
            return not isinstance(count, int) or count > 0

        def apart(eng, waited, index):
            if not isinstance(index, int):
                eng.sem_inc(waited, 1)

        def sweep(eng, turn):
            turn(None, None, 0)
            turn(0, None, 1)
            turn(1, 0, 2)
            with eng.Fori(2, GROUPS - 1) as i:
                turn(i, i - 1, i + 1)
            turn(GROUPS - 1, GROUPS - 2, None)
            turn(None, GROUPS - 1, None)

        block = stack.enter_context(nc.Block())

        @block.sync
        def _(sp):
            def load_xt(i):
                sp.wait_ge(xt_lo_made, i)
                sp.dma_start(xt_in[:], x_t[bass.ds(i, 1)].rearrange("a p k n -> p (a k) n")).then_inc(xt_loaded, 16)

            def load_x(i):
                sp.wait_ge(x_loaded, 16 * i)
                sp.dma_start(x_all[:, bass.ds(i, 1), :], x[bass.ds(i, 1)].rearrange("a p n -> p a n")).then_inc(x_loaded, 16)

            def store(i):
                for p in range(2):
                    cols = slice(2 * p * D, 2 * (p + 1) * D)
                    sp.wait_ge(y_made, 2 * i + p + 1)
                    sp.dma_start(out[bass.ds(i, 1), :, cols].rearrange("a p n -> p a n"),
                                 y[:, 2 * p:2 * p + 2, :].rearrange("p j d -> p (j d)").unsqueeze(1)).then_inc(y_stored, 16)

            sp.dma_start(wqk_in[:], w_qk).then_inc(qk_loaded, 16)
            sp.dma_start(x_all[:, 0, :], x[0]).then_inc(x_loaded, 16)
            sp.dma_start(wvo_in[:], w_vo).then_inc(vo_loaded, 16)
            sp.dma_start(w1_in[:], w1).then_inc(w1_loaded, 16)
            load_xt(1)
            sp.dma_start(w2_in[:], w2).then_inc(w2_loaded, 16)
            load_x(1)
            load_x(2)
            load_xt(2)
            with sp.Fori(3, GROUPS) as i:
                load_x(i)
                load_xt(i)
                store(i - 3)
            with sp.Fori(GROUPS - 3, GROUPS) as i:
                store(i)
            sp.wait_ge(y_stored, 2 * 16 * GROUPS)

        @block.tensor
        def _(pe):
            mm = pe.matmul

            def fold_keys():
                pe.wait_ge(wq_step, 3 * KD)
                for m in range(KD):
                    for k in range(KD):
                        last = mm(z_ps[m][:, 0:D + 1], wk[:, k, m * P:(m + 1) * P], wqk_in[:, k, D:2 * D + 1],
                                  start=k == 0, stop=k == KD - 1)
                    last.then_inc(wkq_ps_made, 1)
                for m in range(KD):
                    for k in range(KD):
                        mm(y_ps[0][:, m:m + 1], wq[:, k, m * P:(m + 1) * P], bk[:, k, :], start=k == 0, stop=k == KD - 1)
                pe.wait_ge(wide_made, 1)
                for k in range(KD):
                    last = mm(y_ps[0][:, KD:KD + 1], bq_wide[:, k, :], bk[:, k, :], start=k == 0, stop=k == KD - 1)
                last.then_inc(bias_ps_made, 1)
                pe.wait_ge(ctx_loaded, 16)

            def keys_of(h):
                key_ps, bias_ps = (tr_ps, y_ps[1]) if h == 0 else (z_ps, y_ps[1])
                for m in range(KD):
                    if h == 1:
                        pe.wait_ge(vals_read, 2 * (m + 1))
                    for k in range(KD):
                        if h == 0:
                            pe.wait_ge(wkq_made, k + 1)
                        last = mm(key_ps[m][:, 0:HALF], wkq[:, k, m * P:(m + 1) * P], ctx_in[:, k, h * HALF:(h + 1) * HALF],
                                  start=k == 0, stop=k == KD - 1)
                    last.then_inc(keys_ps_made, 1)
                if h == 0:
                    pe.wait_ge(kbq_made, 2)
                if h == 1:
                    pe.wait_ge(sbias_made, 1)
                for k in range(KD):
                    last = mm(bias_ps[:, 0:HALF], kbq_wide[:, k, :], ctx_in[:, k, h * HALF:(h + 1) * HALF],
                              start=k == 0, stop=k == KD - 1)
                last.then_inc(sbias_ps_made, 1)

            def fold_values():
                pe.wait_ge(vo_loaded, 16)
                pe.wait_ge(wkq_made, 2)
                for m in range(KD):
                    for k in range(KD):
                        last = mm(z_ps[m][:, 0:D], wv[:, k, m * P:(m + 1) * P], wo_t[:, k, :], start=k == 0, stop=k == KD - 1)
                    last.then_inc(wvo_ps_made, 1)
                pe.wait_ge(wide_made, 2)
                pe.wait_ge(small_loaded, 16)
                pe.wait_ge(bias_made, 1)
                for k in range(KD):
                    mm(y_ps[0][:, 0:D], bv_wide[:, k, :], wo_t[:, k, :], start=k == 0, stop=False)
                pe.wait_ge(consts_made, 2)
                mm(y_ps[0][:, 0:D], row0[:], bo, start=False, stop=True).then_inc(wvo_ps_made, 1)

            def values_of(b):
                if b == 0:
                    pe.wait_ge(rest_made, 3)
                    pe.wait_ge(wvo_made, 3)
                if b == 1:
                    pe.wait_ge(keys_lo_made, 4)
                for n in (2 * b, 2 * b + 1):
                    if b > 0:
                        pe.wait_ge(vals_read, 2 * (n - 1))
                    dst = z_ps[n % 2][:, 0:D]
                    for k in range(KD):
                        rows = ctx_rest[:, k, b, :] if n % 2 else ctx_in[:, k, b * S:b * S + P]
                        mm(dst, rows, wvo[:, k, :], start=k == 0, stop=False)
                    mm(dst, row0[:], vo_bias[:], start=False, stop=True).then_inc(vals_ps_made, 1)

            def scores(a, j):
                if j == 0:
                    pe.wait_ge(xt_lo_made, a + 1)
                if above_zero(TILES * a + j - 1):
                    pe.wait_ge(scaled_made, TILES * a + j - 1)
                at = (a // PER_BATCH) * S
                rows = slice(j * P, (j + 1) * P)
                dst = sc_ps[j % 2][:, 0:S]
                for k in range(KD):
                    mm(dst, xt_hi[:, k, rows], keys_hi[:, k, bass.ds(at, S)], start=k == 0, stop=False)
                    mm(dst, xt_hi[:, k, rows], keys_lo[:, k, bass.ds(at, S)], start=False, stop=False)
                    last = mm(dst, xt_lo[:, k, rows], keys_hi[:, k, bass.ds(at, S)], start=False, stop=k == KD - 1)
                last.then_inc(scores_made, 1)

            def transpose_picked(a, p):
                pe.wait_ge(rest_copied, 2 * a + p + 1)
                if above_zero(2 * (a - 1) + p + 1):
                    pe.wait_ge(x2nt_lo_made, 2 * (a - 1) + p + 1)
                for c in range(2):
                    for t in range(2):
                        last = pe.transpose(tr_ps[p][:, (2 * c + t) * P:(2 * c + t + 1) * P],
                                            picked[:, 2 * p + t, c * P:(c + 1) * P], ident[:])
                last.then_inc(pt_ps_made, 1)

            def attend(a, p):
                pe.wait_ge(pt_lo_made, 4 * a + 2 * p + 2)
                if p == 0:
                    if above_zero(2 * (a - 1)):
                        pe.wait_ge(y_made, 2 * (a - 1))
                else:
                    pe.wait_ge(x2_made, TILES * a + 2)
                b = a // PER_BATCH
                for t in range(2):
                    dst = y_ps[0][:, t * D:(t + 1) * D]
                    rows = slice(t * P, (t + 1) * P)
                    hi, lo, rest = (v[:, bass.ds(b, 1), :].rearrange("p o d -> p (o d)") for v in (vals_hi, vals_lo, vals_rest))
                    mm(dst, pt_hi[:, 0, rows], hi, start=True, stop=False)
                    mm(dst, pt_hi[:, 0, rows], lo, start=False, stop=False)
                    mm(dst, pt_lo[:, rows], hi, start=False, stop=False)
                    last = mm(dst, pt_hi[:, 1, rows], rest, start=False, stop=True)
                last.then_inc(att_made, 1)

            def transpose_x2n(a, p):
                pe.wait_ge(x2n_made, TILES * a + 2 * p + 2)
                pe.wait_ge(pt_lo_made, 4 * a + 2 * p + 2)
                for k in range(KD):
                    for t in range(2):
                        last = pe.transpose(tr_ps[p][:, (2 * k + t) * P:(2 * k + t + 1) * P],
                                            x2n[:, 2 * p + t, k * P:(k + 1) * P], ident[:])
                last.then_inc(x2nt_ps_made, 1)

            def ffn_in(g, c):
                if c == 0:
                    pe.wait_ge(x2nt_lo_made, 2 * g + 2)
                if above_zero(KF * g + c - 1):
                    pe.wait_ge(hid_hi_made, KF * g + c - 1)
                dst = z_ps[c % 2]
                cols = slice(c * P, (c + 1) * P)
                for k in range(KD):
                    mm(dst[:], w1_hi[:, k, cols], x2nt_hi[:, k, :], start=k == 0, stop=False)
                    mm(dst[:], w1_hi[:, k, cols], x2nt_lo[:, k, :], start=False, stop=False)
                    last = mm(dst[:], w1_lo[:, k, cols], x2nt_hi[:, k, :], start=False, stop=k == KD - 1)
                last.then_inc(z_made, 1)

            def ffn_out(a, g, j):
                dst = y_ps[1 - j // 2][:, (j % 2) * D:(j % 2 + 1) * D]
                rows = slice(j * P, (j + 1) * P)
                if j == 0:
                    if isinstance(g, int) and g == 0:
                        pe.wait_ge(w2_lo_made, 1)
                    if above_zero(2 * g - 1):
                        pe.wait_ge(y_made, 2 * g - 1)
                    pe.wait_ge(hid_hi_made, KF * (g + 1))
                if j == 2:
                    pe.wait_ge(x2_made, TILES * (g + 1 if a is None else a + 1))
                    if above_zero(2 * g):
                        pe.wait_ge(y_made, 2 * g)
                for c in range(KF):
                    mm(dst, hid_hi[:, c, rows], w2_hi[:, c, :], start=c == 0, stop=False)
                    mm(dst, hid_hi[:, c, rows], w2_lo[:, c, :], start=False, stop=False)
                if j == 0:
                    pe.wait_ge(hid_lo_made, KF * (g + 1))
                for c in range(KF):
                    last = mm(dst, hid_lo[:, c, rows], w2_hi[:, c, :], start=False, stop=c == KF - 1)
                if j % 2:
                    last.then_inc(ffn_made, 1)

            def turn(a, g, n):
                if a is not None:
                    scores(a, 0)
                    scores(a, 1)
                if g is not None:
                    ffn_in(g, 0)
                    ffn_in(g, 1)
                if a is not None:
                    scores(a, 2)
                    scores(a, 3)
                if g is not None:
                    ffn_in(g, 2)
                    ffn_in(g, 3)
                elif a is not None:
                    fold_values()
                    values_of(0)
                    keys_of(1)
                    values_of(1)
                if a is not None:
                    transpose_picked(a, 0)
                if g is not None:
                    ffn_in(g, 4)
                    ffn_in(g, 5)
                if a is not None:
                    if g is None:
                        pe.wait_ge(vals_lo_made, 2)
                    attend(a, 0)
                    transpose_picked(a, 1)
                    if g is None:
                        values_of(2)
                if g is not None:
                    ffn_in(g, 6)
                    ffn_in(g, 7)
                if a is not None:
                    attend(a, 1)
                if g is not None:
                    ffn_out(a, g, 0)
                    ffn_out(a, g, 1)
                if a is not None:
                    transpose_x2n(a, 0)
                    if g is None:
                        values_of(3)
                if g is not None:
                    ffn_out(a, g, 2)
                if a is not None:
                    transpose_x2n(a, 1)
                    if g is None:
                        pe.wait_ge(w1_lo_made, 1)
                        pe.wait_ge(vals_lo_made, 2 * B)
                        pe.wait_ge(sbias_made, 2)
                if g is not None:
                    ffn_out(a, g, 3)

            fold_keys()
            keys_of(0)
            pe.wait_ge(keys_lo_made, 2)
            sweep(pe, turn)

        @block.scalar
        def _(act):
            func = act.activation
            act.dma_start(ctx_in[:], ctx_t).then_inc(ctx_loaded, 16)
            act.dma_start(xt_in[:], x_t[0]).then_inc(xt_loaded, 16)
            act.dma_start(small_in[:], small).then_inc(small_loaded, 16)

            def keys_to_hi(h):
                key_ps = tr_ps if h == 0 else z_ps
                if h == 0:
                    act.wait_ge(bias_made, 1)
                for m in range(KD):
                    act.wait_ge(keys_ps_made, KD * h + m + 1)
                    func(keys_hi[:, m, h * HALF:(h + 1) * HALF], key_ps[m][:, 0:HALF], ACT.Identity,
                         bias=key_bias[:, m:m + 1]).then_inc(keys_hi_made, 1)
                act.wait_ge(sbias_ps_made, h + 1)
                func(score_bias[:, h * HALF:(h + 1) * HALF], y_ps[1][:, 0:HALF], ACT.Identity,
                     bias=key_bias[:, KD:KD + 1]).then_inc(sbias_made, 1)

            def take_tanh():
                act.wait_ge(small_loaded, 16)
                func(tanh_g[:], small_in[:, 0:2], ACT.Tanh).then_inc(tanh_made, 1)

            def fold_wvo():
                act.wait_ge(tanh_made, 1)
                for m in range(KD):
                    act.wait_ge(wvo_ps_made, m + 1)
                    func(wvo[:, m, :], z_ps[m][:, 0:D], ACT.Identity, scale=tanh_g[:, 0:1]).then_inc(wvo_made, 1)
                act.wait_ge(wvo_ps_made, 3)
                func(vo_bias[:], y_ps[0][:, 0:D], ACT.Identity, scale=tanh_g[:, 0:1]).then_inc(wvo_made, 1)

            def split_values(n):
                b = n // 2
                act.wait_ge(vals_ps_made, n + 1)
                if above_zero(n - 3):
                    act.wait_ge(vals_lo_made, n - 3)
                func(values[:, n % 2, b % 2, :], z_ps[n % 2][:, 0:D], ACT.Copy).then_inc(vals_read, 1)
                hi = vals_rest if n % 2 else vals_hi
                func(hi[:, b, :], z_ps[n % 2][:, 0:D], ACT.Copy).then_inc(vals_read, 1)

            def w1_to_hi():
                act.wait_ge(w1_loaded, 16)
                func(w1_hi[:], w1_in[:], ACT.Copy).then_inc(w1_hi_made, 1)

            def w2_to_hi():
                act.wait_ge(w2_loaded, 16)
                func(w2_hi[:], w2_in[:], ACT.Identity, scale=tanh_g[:, 1:2]).then_inc(w2_hi_made, 1)
                func(w2_in[:], w2_in[:], ACT.Identity, scale=tanh_g[:, 1:2]).then_inc(w2_hi_made, 1)

            def xt_to_hi(n):
                act.wait_ge(xt_loaded, 16 * (n + 1))
                if above_zero(TILES * n):
                    act.wait_ge(scores_made, TILES * n)
                func(xt_hi[:], xt_in[:], ACT.Copy).then_inc(xt_hi_made, 1)

            def exps(a, p):
                for t in range(2):
                    j = 2 * p + t
                    act.wait_ge(topk_step, (2 * a + p) * STEPS + 3)
                    func(probs[:, j, :], score[:, j, :], ACT.Exp, bias=neg_max[:, j:j + 1], scale=SCALE).then_inc(probs_made, 1)

            def copy_rest(a, p):
                act.wait_ge(picked_made, TILES * a + 2 * p + 2)
                rest = picked[:, 2 * p:2 * p + 2, P:2 * P].rearrange("p j (r c) -> p j r c", c=32)
                func(rest[:, :, 1:3, 0:SR], rest[:, :, 0:1, 0:SR].to_broadcast([P, 2, 2, SR]), ACT.Copy).then_inc(rest_copied, 1)

            def pt_to_hi(a, p):
                act.wait_ge(pt_ps_made, 2 * a + p + 1)
                if above_zero(2 * a + p):
                    act.wait_ge(att_made, 2 * a + p)
                func(pt_hi[:], tr_ps[p][:].rearrange("p (k c) -> p k c", k=2), ACT.Copy).then_inc(pt_hi_made, 1)

            def x2nt_to_hi(a, p):
                act.wait_ge(x2nt_ps_made, 2 * a + p + 1)
                func(x2nt_hi[:, :, 2 * p * P:2 * (p + 1) * P], tr_ps[p][:].rearrange("p (k c) -> p k c", k=KD),
                     ACT.Copy).then_inc(x2nt_hi_made, 1)

            def relu(g, c):
                act.wait_ge(z_made, KF * g + c + 1)
                if above_zero(KF * g + c - 1):
                    act.wait_ge(hid_lo_made, KF * g + c - 1)
                func(hid[:, c % 2, :], z_ps[c % 2][:], ACT.Relu, bias=b1[:, c:c + 1]).then_inc(hid_made, 1)
                func(hid_hi[:, c, :], z_ps[c % 2][:], ACT.Relu, bias=b1[:, c:c + 1]).then_inc(hid_hi_made, 1)

            def turn(a, g, n):
                if a is None and n is not None:
                    xt_to_hi(n)
                    keys_to_hi(0)
                    take_tanh()
                if g is not None:
                    relu(g, 0)
                if a is not None:
                    if g is None:
                        w1_to_hi()
                    exps(a, 0)
                    if g is None:
                        fold_wvo()
                        split_values(0)
                        split_values(1)
                        keys_to_hi(1)
                if g is not None:
                    relu(g, 1)
                if a is not None:
                    copy_rest(a, 0)
                if g is not None:
                    relu(g, 2)
                if a is not None:
                    exps(a, 1)
                    if g is None:
                        split_values(2)
                        split_values(3)
                if g is not None:
                    relu(g, 3)
                if a is not None:
                    pt_to_hi(a, 0)
                if g is not None:
                    relu(g, 4)
                    relu(g, 5)
                if a is not None:
                    copy_rest(a, 1)
                    pt_to_hi(a, 1)
                    if g is None:
                        split_values(4)
                        split_values(5)
                        w2_to_hi()
                if g is not None:
                    relu(g, 6)
                    relu(g, 7)
                if a is not None and n is not None:
                    xt_to_hi(n)
                if a is not None:
                    x2nt_to_hi(a, 0)
                    if g is None:
                        split_values(6)
                        split_values(7)
                    x2nt_to_hi(a, 1)

            sweep(act, turn)

        @block.vector
        def _(dve):
            def fold_keys():
                nc.vector.memset(ones[:], 1.0).then_inc(vector_zeroed, 1)
                dve.wait_ge(qk_loaded, 16)
                for k in range(KD):
                    nc.vector.bn_stats(wq_stats[:, k, :], wq[:, k, :]).then_inc(wq_step, 1)
                for k in range(KD):
                    dve.wait_ge(wq_step, k + 1)
                    nc.vector.bn_aggr(wq_mean[:, k, :], wq_stats[:, k, :]).then_inc(wq_step, 1)
                for k in range(KD):
                    dve.wait_ge(wq_step, KD + k + 1)
                    nc.vector.tensor_scalar(wq[:, k, :], wq[:, k, :], wq_mean[:, k, 0:1], None, ALU.subtract).then_inc(wq_step, 1)
                dve.wait_ge(vector_zeroed, 1)
                for k in range(KD):
                    last = nc.vector.tensor_scalar(bq_wide[:, k, :], ones[:], bq[:, k, :], None, ALU.mult)
                last.then_inc(wide_made, 1)
                nc.vector.memset(picked[:], 0.0).then_inc(vector_zeroed, 1)
                for m in range(KD):
                    dve.wait_ge(wkq_ps_made, m + 1)
                    nc.vector.tensor_copy(wkq[:, m, :], z_ps[m][:, 0:D + 1]).then_inc(wkq_made, 1)
                for m in range(KD):
                    dve.wait_ge(wkq_made, m + 1)
                    nc.vector.tensor_scalar(kbq_wide[:, m, :], ones[:], wkq[:, m, D:D + 1], None, ALU.mult).then_inc(kbq_made, 1)
                dve.wait_ge(bias_ps_made, 1)
                nc.vector.tensor_copy(key_bias[:], y_ps[0][:, 0:KD + 1]).then_inc(bias_made, 1)

            def keys_to_lo(h):
                key_ps = tr_ps if h == 0 else z_ps
                cols = slice(h * HALF, (h + 1) * HALF)
                dve.wait_ge(bias_made, 1)
                for m in range(KD):
                    dve.wait_ge(keys_hi_made, KD * h + m + 1)
                    nc.vector.scalar_tensor_tensor(keys_lo[:, m, cols], key_ps[m][:, 0:HALF], key_bias[:, m:m + 1],
                                                   keys_hi[:, m, cols], ALU.add, ALU.subtract).then_inc(keys_lo_made, 1)

            def widen_bv():
                dve.wait_ge(vo_loaded, 16)
                for k in range(KD):
                    last = nc.vector.tensor_scalar(bv_wide[:, k, :], ones[:], bv[:, k, :], None, ALU.mult)
                last.then_inc(wide_made, 1)

            def w2_to_lo():
                dve.wait_ge(w2_hi_made, 2)
                nc.vector.tensor_tensor(w2_lo[:], w2_in[:], w2_hi[:], ALU.subtract).then_inc(w2_lo_made, 1)

            def stats_x(n):
                dve.wait_ge(x_loaded, 16 * (n + 1))
                if above_zero(2 * n):
                    dve.wait_ge(norm1_step, 2 * n)
                apart(dve, vector_waited, n)
                for j in range(TILES):
                    rows = x_all[:, bass.ds(n, 1), j * D:(j + 1) * D].rearrange("p o d -> p (o d)")
                    nc.vector.bn_stats(stats1[:, j, :], rows).then_inc(stats1_step, 1)
                for j in range(TILES):
                    dve.wait_ge(stats1_step, 2 * TILES * n + j + 1)
                    apart(dve, vector_waited, n)
                    nc.vector.bn_aggr(mv1[:, j, :], stats1[:, j, :]).then_inc(stats1_step, 1)

            def xt_to_lo(n):
                dve.wait_ge(xt_hi_made, n + 1)
                nc.vector.tensor_tensor(xt_lo[:], xt_in[:], xt_hi[:], ALU.subtract).then_inc(xt_lo_made, 1)

            def scale_scores(a, p):
                at = (a // PER_BATCH) * S
                for t in range(2):
                    j = 2 * p + t
                    dve.wait_ge(scores_made, TILES * a + j + 1)
                    if j == 0:
                        dve.wait_ge(norm1_step, 2 * (a + 1))
                    if above_zero(TILES * (a - 1) + j + 1):
                        dve.wait_ge(probs_made, TILES * (a - 1) + j + 1)
                    nc.vector.scalar_tensor_tensor(score[:, j, :], sc_ps[t][:, 0:S], norm1[:, 1, j:j + 1],
                                                   score_bias[:, bass.ds(at, S)], ALU.mult, ALU.add).then_inc(scaled_made, 1)

            def topk_round(a, p, r):
                done = (2 * a + p) * STEPS
                at = 0 if r == 0 else 4 * r + 1
                for t in range(2):
                    j = 2 * p + t
                    if r == 0:
                        dve.wait_ge(scaled_made, TILES * a + j + 1)
                    else:
                        dve.wait_ge(topk_step, done + at - 1 + t)
                    apart(dve, vector_waited, a)
                    nc.vector.max(top[:, j, 8 * r:8 * r + 8], score[:, j, :] if r == 0 else left[:, j, :]).then_inc(topk_step, 1)
                if r == 0:
                    dve.wait_ge(topk_step, done + 2)
                    nc.vector.tensor_scalar(neg_max[:, 2 * p:2 * p + 2], top[:, 2 * p:2 * p + 2, 0], -SCALE, None,
                                            ALU.mult).then_inc(topk_step, 1)
                for t in range(2):
                    j = 2 * p + t
                    dve.wait_ge(topk_step, done + at + 1 + t)
                    apart(dve, vector_waited, a)
                    nc.vector.match_replace(left[:, j, :], top[:, j, 8 * r:8 * r + 8], score[:, j, :] if r == 0 else left[:, j, :],
                                            TAKEN).then_inc(topk_step, 1)

            def pick(a, p):
                for t in range(2):
                    j = 2 * p + t
                    dve.wait_ge(topk_step, (2 * a + p) * STEPS + STEPS - 1 + t)
                    dve.wait_ge(probs_made, TILES * a + j + 1)
                    nc.vector.scalar_tensor_tensor(picked[:, j, 0:S], left[:, j, :], TAKEN, probs[:, j, :], ALU.is_equal, ALU.mult,
                                                   accum_out=denom[:, j:j + 1]).then_inc(picked_made, 1)

            def invert(a, p):
                dve.wait_ge(picked_made, TILES * a + 2 * p + 2)
                nc.vector.reciprocal(inv_denom[:, 2 * p:2 * p + 2], denom[:, 2 * p:2 * p + 2]).then_inc(inv_made, 1)

            def pt_to_lo(a, p):
                dve.wait_ge(pt_hi_made, 2 * a + p + 1)
                nc.vector.tensor_tensor(pt_lo[:], tr_ps[p][:, 0:2 * P], pt_hi[:, 0, :], ALU.subtract).then_inc(pt_lo_made, 1)
                nc.vector.tensor_tensor(pt_hi[32:64, 1, :], tr_ps[p][32:64, 2 * P:4 * P], pt_hi[32:64, 1, :],
                                        ALU.subtract).then_inc(pt_lo_made, 1)

            def residual(a, p):
                dve.wait_ge(att_made, 2 * a + p + 1)
                dve.wait_ge(inv_made, 2 * a + p + 1)
                if above_zero(2 * (a - 1) + p + 1):
                    dve.wait_ge(x2b_made, 2 * (a - 1) + p + 1)
                apart(dve, vector_waited, a)
                for t in range(2):
                    j = 2 * p + t
                    rows = x_all[:, bass.ds(a, 1), j * D:(j + 1) * D].rearrange("p o d -> p (o d)")
                    nc.vector.scalar_tensor_tensor(x2[:, j, :], y_ps[0][:, t * D:(t + 1) * D], inv_denom[:, j:j + 1], rows,
                                                   ALU.mult, ALU.add).then_inc(x2_made, 1)
                for t in range(2):
                    j = 2 * p + t
                    dve.wait_ge(x2_made, TILES * a + j + 1)
                    nc.vector.bn_stats(stats2[:, j, :], x2[:, j, :]).then_inc(stats2_step, 1)
                for t in range(2):
                    j = 2 * p + t
                    dve.wait_ge(stats2_step, 2 * TILES * a + 4 * p + t + 1)
                    apart(dve, vector_waited, a)
                    nc.vector.bn_aggr(mv2[:, j, :], stats2[:, j, :]).then_inc(stats2_step, 1)

            def x2nt_to_lo(a, p):
                dve.wait_ge(x2nt_hi_made, 2 * a + p + 1)
                cols = slice(2 * p * P, 2 * (p + 1) * P)
                nc.vector.tensor_tensor(x2nt_lo[:, :, cols], tr_ps[p][:].rearrange("p (k c) -> p k c", k=KD),
                                        x2nt_hi[:, :, cols], ALU.subtract).then_inc(x2nt_lo_made, 1)

            def output(g, p):
                dve.wait_ge(ffn_made, 2 * g + p + 1)
                dve.wait_ge(x2b_made, 2 * g + 2)
                if above_zero(32 * g):
                    dve.wait_ge(y_stored, 32 * g)
                nc.vector.tensor_tensor(y[:, 2 * p:2 * p + 2, :], y_ps[1 - p][:].rearrange("p (j d) -> p j d", j=2),
                                        x2b[:, 2 * p:2 * p + 2, :], ALU.add).then_inc(y_made, 1)

            def turn(a, g, n):
                if a is None and n is not None:
                    stats_x(n)
                    xt_to_lo(n)
                    keys_to_lo(0)
                    widen_bv()
                    dve.wait_ge(sbias_made, 1)
                    dve.wait_ge(vector_zeroed, 2)
                if a is not None:
                    scale_scores(a, 0)
                    for r in range(ROUNDS):
                        topk_round(a, 0, r)
                    pick(a, 0)
                    invert(a, 0)
                    scale_scores(a, 1)
                    topk_round(a, 1, 0)
                    if g is None:
                        keys_to_lo(1)
                    topk_round(a, 1, 1)
                    pt_to_lo(a, 0)
                    topk_round(a, 1, 2)
                    topk_round(a, 1, 3)
                    pick(a, 1)
                    invert(a, 1)
                    residual(a, 0)
                    pt_to_lo(a, 1)
                if a is not None and n is not None:
                    stats_x(n)
                    xt_to_lo(n)
                if a is not None:
                    residual(a, 1)
                if g is not None:
                    output(g, 0)
                if a is not None:
                    x2nt_to_lo(a, 0)
                    if g is None:
                        w2_to_lo()
                        dve.wait_ge(sbias_made, 2)
                    x2nt_to_lo(a, 1)
                if g is not None:
                    output(g, 1)

            fold_keys()
            sweep(dve, turn)

        @block.gpsimd
        def _(pool):
            def prepare():
                nc.gpsimd.memset(ident[:], 0.0).then_inc(pool_zeroed, 1)
                nc.gpsimd.memset(row0[:], 0.0).then_inc(pool_zeroed, 1)
                nc.gpsimd.memset(ctx_rest[:], 0.0).then_inc(pool_zeroed, 1)
                nc.gpsimd.memset(neg_half[:], -0.5).then_inc(pool_zeroed, 1)
                pool.wait_ge(pool_zeroed, 4)
                nc.gpsimd.affine_select(out=ident[:], in_=ident[:], compare_op=ALU.not_equal, fill=1.0, base=0,
                                        pattern=[[-1, P]], channel_multiplier=1).then_inc(consts_made, 1)
                nc.gpsimd.memset(row0[0:1, :], 1.0).then_inc(consts_made, 1)

            def stack_rest():
                pool.wait_ge(ctx_loaded, 16)
                by_batch = ctx_in[:].rearrange("p k (b s) -> p k b s", b=B)
                for r in range(3):
                    for k in range(KD):
                        last = nc.gpsimd.tensor_copy(ctx_rest[:, k, :, 32 * r:32 * r + SR], by_batch[:, k, :, P:S])
                    last.then_inc(rest_made, 1)

            def values_to_lo(n):
                pool.wait_ge(vals_read, 2 * n + 2)
                if above_zero(n):
                    pool.wait_ge(vals_lo_made, n)
                b = n // 2
                if n % 2:
                    nc.gpsimd.tensor_tensor(vals_rest[64:96, b, :], values[64:96, 1, b % 2, :], vals_rest[64:96, b, :],
                                            ALU.subtract).then_inc(vals_lo_made, 1)
                else:
                    nc.gpsimd.tensor_tensor(vals_lo[:, b, :], values[:, 0, b % 2, :], vals_hi[:, b, :],
                                            ALU.subtract).then_inc(vals_lo_made, 1)

            def w1_to_lo():
                pool.wait_ge(w1_hi_made, 1)
                nc.gpsimd.tensor_tensor(w1_lo[:], w1_in[:], w1_hi[:], ALU.subtract).then_inc(w1_lo_made, 1)

            def scale_b2():
                pool.wait_ge(tanh_made, 1)
                for t in range(2):
                    nc.gpsimd.tensor_scalar(b2_pair[:, t, :], b2, tanh_g[:, 1:2], 1.0, ALU.mult, ALU.mult).then_inc(b2_made, 1)

            def rstd_x(n):
                pool.wait_ge(stats1_step, 2 * TILES * (n + 1))
                if above_zero(TILES * n):
                    pool.wait_ge(scaled_made, TILES * n)
                apart(pool, pool_waited, n)
                nc.gpsimd.tensor_scalar(norm1[:, 0, :], mv1[:, :, 1], EPS, 1.0, ALU.add, ALU.mult).then_inc(norm1_step, 1)
                pool.wait_ge(norm1_step, 2 * n + 1)
                nc.gpsimd.tensor_tensor(norm1[:, 1, :], norm1[:, 0, :], neg_half[:], ALU.pow).then_inc(norm1_step, 1)

            def normalise_x2(a, p):
                cols = slice(2 * p, 2 * p + 2)
                pool.wait_ge(stats2_step, 2 * TILES * a + 4 * p + 4)
                apart(pool, pool_waited, a)
                nc.gpsimd.tensor_scalar(norm2[:, 0, cols], mv2[:, cols, 1], EPS, 1.0, ALU.add, ALU.mult).then_inc(norm2_step, 1)
                nc.gpsimd.tensor_scalar(norm2[:, 1, cols], mv2[:, cols, 0], -1.0, 0.0, ALU.mult, ALU.add).then_inc(norm2_step, 1)
                pool.wait_ge(norm2_step, 6 * a + 3 * p + 1)
                nc.gpsimd.tensor_tensor(norm2[:, 2, cols], norm2[:, 0, cols], neg_half[:, 0:2], ALU.pow).then_inc(norm2_step, 1)
                pool.wait_ge(norm2_step, 6 * a + 3 * p + 3)
                if above_zero(2 * (a - 1) + p + 1):
                    pool.wait_ge(x2nt_ps_made, 2 * (a - 1) + p + 1)
                apart(pool, pool_waited, a)
                for t in range(2):
                    j = 2 * p + t
                    nc.gpsimd.tensor_scalar(x2n[:, j, :], x2[:, j, :], norm2[:, 1, j:j + 1], norm2[:, 2, j:j + 1],
                                            ALU.add, ALU.mult).then_inc(x2n_made, 1)

            def add_b2(g):
                for p in range(2):
                    if above_zero(2 * (g - 1) + p + 1):
                        pool.wait_ge(y_made, 2 * (g - 1) + p + 1)
                    pool.wait_ge(x2_made, TILES * g + 2 * p + 2)
                    pair = slice(2 * p, 2 * p + 2)
                    nc.gpsimd.tensor_tensor(x2b[:, pair, :], x2[:, pair, :], b2_pair[:], ALU.add).then_inc(x2b_made, 1)

            def hid_to_lo(g, c):
                pool.wait_ge(hid_hi_made, KF * g + c + 1)
                pool.wait_ge(hid_made, KF * g + c + 1)
                if above_zero(2 * g):
                    pool.wait_ge(ffn_made, 2 * g)
                nc.gpsimd.tensor_tensor(hid_lo[:, c, :], hid[:, c % 2, :], hid_hi[:, c, :], ALU.subtract).then_inc(hid_lo_made, 1)

            def turn(a, g, n):
                if a is None and n is not None:
                    rstd_x(n)
                    stack_rest()
                    scale_b2()
                if a is not None and g is None:
                    w1_to_lo()
                    for n_out in range(4):
                        values_to_lo(n_out)
                if g is not None:
                    add_b2(g)
                    for c in range(KF):
                        hid_to_lo(g, c)
                if a is not None:
                    if g is None:
                        pool.wait_ge(vals_lo_made, 4)
                    normalise_x2(a, 0)
                    if g is None:
                        values_to_lo(4)
                        values_to_lo(5)
                        pool.wait_ge(vals_lo_made, 6)
                    if n is not None:
                        rstd_x(n)
                    normalise_x2(a, 1)
                    if g is None:
                        values_to_lo(6)
                        values_to_lo(7)
                        pool.wait_ge(vals_lo_made, 8)

            prepare()
            sweep(pool, turn)


def kernel(x, ctx_1024, g_xattn, g_ffn, L0_xattn_Wq, L0_xattn_bq, L0_xattn_Wk, L0_xattn_bk, L0_xattn_Wv, L0_xattn_bv,
           L0_xattn_Wo, L0_xattn_bo, L0_ffn_W1, L0_ffn_b1, L0_ffn_W2, L0_ffn_b2):
    import numpy as np
    import concourse.bacc as bacc
    from concourse.bass_utils import run_bass_kernel_spmd

    def by_partition(a):
        a = np.asarray(a)
        return a.reshape(-1, P, a.shape[-1]).transpose(1, 0, 2)

    def column(v):
        return by_partition(np.asarray(v)[:, None])

    def everywhere(v):
        v = np.asarray(v)
        return np.broadcast_to(v, (P, v.size))

    ctx_rows = np.asarray(ctx_1024).reshape(B * S, D)
    arrays = {
        "x": np.asarray(x).reshape(GROUPS, P, TILES * D),
        "x_t": np.asarray(x).reshape(GROUPS, P, TILES, KD, P).transpose(0, 4, 3, 2, 1).reshape(GROUPS, P, KD, GROUP),
        "w_qk": np.concatenate([by_partition(L0_xattn_Wk), by_partition(L0_xattn_Wq), column(L0_xattn_bq), column(L0_xattn_bk)], axis=2),
        "ctx_t": by_partition(ctx_rows.T),
        "w_vo": np.concatenate([by_partition(L0_xattn_Wv), by_partition(np.asarray(L0_xattn_Wo).T), column(L0_xattn_bv)], axis=2),
        "small": np.concatenate([everywhere(g_xattn), everywhere(g_ffn), np.asarray(L0_ffn_b1).reshape(KF, P).T,
                                 everywhere(L0_xattn_bo), everywhere(L0_ffn_b2)], axis=1),
        "w1": by_partition(L0_ffn_W1),
        "w2": by_partition(L0_ffn_W2),
    }
    arrays = {k: np.ascontiguousarray(v) for k, v in arrays.items()}
    nc = bacc.Bacc("TRN2", target_bir_lowering=False, num_devices=1)
    args = [nc.dram_tensor(k, v.shape, mybir.dt.float32, kind="ExternalInput").ap() for k, v in arrays.items()]
    out = nc.dram_tensor("out", (GROUPS, P, TILES * D), mybir.dt.float32, kind="ExternalOutput").ap()
    gated_block(nc, *args, out)
    r = run_bass_kernel_spmd(nc, [arrays], core_ids=[0])
    return r.results[0]["out"].reshape(B, T, D)
```

```python
import concourse.bass as bass
from concourse import mybir
from contextlib import ExitStack

B, T, S, D, F = 4, 1024, 154, 256, 1024
P = 128
TILES = 4
GROUP = TILES * P
GROUPS = B * T // GROUP
PER_BATCH = T // GROUP
KD = D // P
KF = F // P
HID_RING = 4
SR = S - P
TOPK = 32
ROUNDS = TOPK // 8
STEPS = 4 * ROUNDS + 1
SCALE = float(D) ** -0.5
EPS = 1e-5
WARM_UPS = 7
TAKEN = -3.4e38
PIECES = [(0, S), (S, B * S)]


def gated_block(nc, x, x_t, w_k, w_q, ctx_t, w_vo, small, w1, w2, out):
    f32, f32r = mybir.dt.float32, mybir.dt.float32r
    ALU, ACT = mybir.AluOpType, mybir.ActivationFunctionType

    stack = ExitStack()
    with stack:
        def sb(name, shape, dt=f32):
            return stack.enter_context(nc.sbuf_tensor(name, shape, dt))

        def bank(name):
            return stack.enter_context(nc.psum_tensor(name, [P, 512], f32))

        def sem(name):
            return stack.enter_context(nc.semaphore(name))

        with ExitStack() as early:
            def sb_early(name, shape, dt=f32):
                return early.enter_context(nc.sbuf_tensor(name, shape, dt))

            wk_in = sb_early("wk_in", [P, KD, D + 1])
            wq_in = sb_early("wq_in", [P, KD, D + 1])
            ctx_in = sb_early("ctx_in", [P, KD, B * S])
            wvo_in = sb_early("wvo_in", [P, KD, 2 * D + 1])
            bq_wide = sb_early("bq_wide", [P, KD, P])
            bv_wide = sb_early("bv_wide", [P, KD, P])
            k_proj = sb_early("k_proj", [P, KD, B * S])
            keys_f32 = sb_early("keys_f32", [P, KD, (B - 1) * S])
            first_rest = sb_early("first_rest", [P, KD, P])
            other_rest = sb_early("other_rest", [P, KD, P])
            w1_in = sb_early("w1_in", [P, KD, F])

        x2b = sb("x2b", [P, TILES, D])
        hid = sb("hid", [P, HID_RING, GROUP])
        hid_hi = sb("hid_hi", [P, KF, GROUP], f32r)
        hid_lo = sb("hid_lo", [P, KF, GROUP], f32r)
        w2_in = sb("w2_in", [P, KF, D])
        x_all = sb("x_all", [P, GROUPS, TILES * D])
        small_in = sb("small_in", [P, 2 + KF + 2 * D])
        wk_t, bk = wk_in[:, :, 0:D], wk_in[:, :, D:D + 1]
        wq, bq = wq_in[:, :, 0:D], wq_in[:, :, D:D + 1]
        wv, wo_t, bv = wvo_in[:, :, 0:D], wvo_in[:, :, D:2 * D], wvo_in[:, :, 2 * D:2 * D + 1]
        b1 = small_in[:, 2:2 + KF]
        bo = small_in[:, 2 + KF:2 + KF + D]
        b2 = small_in[:, 2 + KF + D:2 + KF + 2 * D]

        ident = sb("ident", [P, P])
        ones = sb("ones", [P, P])
        neg_half = sb("neg_half", [P, TILES])

        tanh_g = sb("tanh_g", [P, 2])
        keys = sb("keys", [P, KD, B * 2 * S], f32r)
        keys_by_batch = keys[:].rearrange("p k (b h s) -> p k b h s", b=B, h=2)
        score_bias = sb("score_bias", [P, B * S])
        wq_stats = sb("wq_stats", [P, KD, 6])
        wq_mean = sb("wq_mean", [P, KD, 2])
        wvo = sb("wvo", [P, KD, D])
        vo_part = sb("vo_part", [P, 2, D])
        vo_bias = sb("vo_bias", [P, D])
        values = sb("values", [P, B + 2, D])
        vals_hi = sb("vals_hi", [P, B, D], f32r)
        vals_lo = sb("vals_lo", [P, B, D], f32r)
        vals_rest = sb("vals_rest", [P, B, D], f32r)
        stacked = sb("stacked", [96, B - 1, D])
        w1_hi = sb("w1_hi", [P, KD, F], f32r)
        w1_lo = sb("w1_lo", [P, KD, F], f32r)
        w2_hi = sb("w2_hi", [P, KF, D], f32r)
        w2_lo = sb("w2_lo", [P, KF, D], f32r)
        b2_pair = sb("b2_pair", [P, 2, D])

        stats1 = sb("stats1", [P, TILES, 6])
        mv1 = sb("mv1", [P, TILES, 2])
        norm1 = sb("norm1", [P, 2, TILES])
        xt_in = sb("xt_in", [P, KD, GROUP])
        xt_hi = sb("xt_hi", [P, KD, GROUP], f32r)
        xt_lo = sb("xt_lo", [P, KD, GROUP], f32r)
        score = sb("score", [P, TILES, S])
        top = sb("top", [P, TILES, TOPK])
        neg_max = sb("neg_max", [P, TILES])
        left = sb("left", [P, TILES, S])
        probs = sb("probs", [P, TILES, S])
        picked = sb("picked", [P, TILES, 2 * P])
        denom = sb("denom", [P, TILES])
        inv_denom = sb("inv_denom", [P, TILES])
        pt_hi = sb("pt_hi", [P, 2, 2 * P], f32r)
        pt_lo = sb("pt_lo", [P, 2 * P], f32r)
        x2 = sb("x2", [P, TILES, D])
        stats2 = sb("stats2", [P, TILES, 6])
        mv2 = sb("mv2", [P, TILES, 2])
        norm2 = sb("norm2", [P, 3, TILES])
        x2n = sb("x2n", [P, TILES, D])
        x2nt_hi = sb("x2nt_hi", [P, KD, GROUP], f32r)
        x2nt_lo = sb("x2nt_lo", [P, KD, GROUP], f32r)
        y = sb("y", [P, TILES, D])

        z_ps = [bank("z_ps0"), bank("z_ps1")]
        tr_ps = [bank("tr_ps0"), bank("tr_ps1")]
        sc_ps = [bank("sc_ps0"), bank("sc_ps1")]
        y_ps = [bank("y_ps0"), bank("y_ps1")]
        last_z_ps = z_ps + sc_ps
        k_ps = [z_ps, [y_ps[1], tr_ps[1]]]
        key_ps = [tr_ps, z_ps]

        k_loaded, q_loaded, vo_loaded, small_loaded = sem("k_loaded"), sem("q_loaded"), sem("vo_loaded"), sem("small_loaded")
        ctx_loaded = [sem("ctx_first_loaded"), sem("ctx_others_loaded")]
        w1_loaded, w2_loaded, x_loaded, xt_loaded = sem("w1_loaded"), sem("w2_loaded"), sem("x_loaded"), sem("xt_loaded")
        first_xt_loaded = sem("first_xt_loaded")
        vector_zeroed, pool_zeroed, neg_half_made = sem("vector_zeroed"), sem("pool_zeroed"), sem("neg_half_made")
        consts_made = sem("consts_made")
        tanh_made = sem("tanh_made")
        wide_made = sem("wide_made")
        k_proj_ps_made, k_proj_made = sem("k_proj_ps_made"), sem("k_proj_made")
        keys_ps_made, keys_hi_made, keys_lo_made = sem("keys_ps_made"), sem("keys_hi_made"), sem("keys_lo_made")
        keys_copied, other_keys_lo_made = sem("keys_copied"), sem("other_keys_lo_made")
        wq_step, sbias_ps_made, sbias_made = sem("wq_step"), sem("sbias_ps_made"), sem("sbias_made")
        rest_made = sem("rest_made")
        wvo_ps_made, wvo_made = sem("wvo_ps_made"), sem("wvo_made")
        bo_scaled, bv_scaled, vo_bias_made = sem("bo_scaled"), sem("bv_scaled"), sem("vo_bias_made")
        vals_ps_made, vals_copied = sem("vals_ps_made"), sem("vals_copied")
        first_biased, others_biased = sem("first_biased"), sem("others_biased")
        vals_hi_made, vals_lo_made = sem("vals_hi_made"), sem("vals_lo_made")
        rest_moved = sem("rest_moved")
        w1_hi_made, w2_hi_made, b2_made = sem("w1_hi_made"), sem("w2_hi_made"), sem("b2_made")
        w1_lo_made, w2_lo_made = sem("w1_lo_made"), sem("w2_lo_made")
        stats1_step, norm1_step = sem("stats1_step"), sem("norm1_step")
        xt_hi_made, xt_lo_made = sem("xt_hi_made"), sem("xt_lo_made")
        first_xt_hi_made, first_xt_lo_made = sem("first_xt_hi_made"), sem("first_xt_lo_made")
        scores_made, scaled_part, scaled_made = sem("scores_made"), sem("scaled_part"), sem("scaled_made")
        topk_step, probs_made = sem("topk_step"), sem("probs_made")
        picked_made, rest_copied, inv_made = sem("picked_made"), sem("rest_copied"), sem("inv_made")
        pt_ps_made, pt_hi_made, pt_lo_made, att_made = sem("pt_ps_made"), sem("pt_hi_made"), sem("pt_lo_made"), sem("att_made")
        x2_made, stats2_step, norm2_step, x2n_made = sem("x2_made"), sem("stats2_step"), sem("norm2_step"), sem("x2n_made")
        x2nt_ps_made, x2nt_hi_made, x2nt_lo_made = sem("x2nt_ps_made"), sem("x2nt_hi_made"), sem("x2nt_lo_made")
        z_made, hid_made, hid_hi_made = sem("z_made"), sem("hid_made"), sem("hid_hi_made")
        hid_lo_made, last_lo_made = sem("hid_lo_made"), sem("last_lo_made")
        x2b_made, ffn_made, y_made, y_stored = sem("x2b_made"), sem("ffn_made"), sem("y_made"), sem("y_stored")
        last_y_made = sem("last_y_made")
        vector_waited, pool_waited = sem("vector_waited"), sem("pool_waited")

        def above_zero(count):
            return not isinstance(count, int) or count > 0

        def apart(eng, waited, index):
            if not isinstance(index, int):
                eng.sem_inc(waited, 1)

        def sweep(eng, turn):
            turn(None, None, 0)
            turn(0, None, 1)
            turn(1, 0, 2)
            with eng.Fori(2, GROUPS - 1) as i:
                turn(i, i - 1, i + 1)
            turn(GROUPS - 1, GROUPS - 2, None)
            turn(None, GROUPS - 1, None)

        block = stack.enter_context(nc.Block())

        @block.sync
        def _(sp):
            def load_xt(i):
                if isinstance(i, int) and i == 1:
                    sp.wait_ge(first_xt_lo_made, 2)
                else:
                    sp.wait_ge(xt_lo_made, i - 1)
                sp.dma_start(xt_in[:], x_t[bass.ds(i, 1)].rearrange("a p k n -> p (a k) n")).then_inc(xt_loaded, 16)

            def load_x(i):
                sp.wait_ge(x_loaded, 16 * i)
                sp.dma_start(x_all[:, bass.ds(i, 1), :], x[bass.ds(i, 1)].rearrange("a p n -> p a n")).then_inc(x_loaded, 16)

            def store(i, p):
                cols = slice(2 * p * D, 2 * (p + 1) * D)
                sp.wait_ge(y_made, 2 * i + p + 1)
                sp.dma_start(out[bass.ds(i, 1), :, cols].rearrange("a p n -> p a n"),
                             y[:, 2 * p:2 * p + 2, :].rearrange("p j d -> p (j d)").unsqueeze(1)).then_inc(y_stored, 16)

            sp.dma_start(wk_in[:], w_k).then_inc(k_loaded, 16)
            sp.dma_start(wq_in[:], w_q).then_inc(q_loaded, 16)
            sp.dma_start(xt_in[:, :, 0:2 * P], x_t[0, :, :, 0:2 * P]).then_inc(first_xt_loaded, 16)
            sp.dma_start(x_all[:, 0, :], x[0]).then_inc(x_loaded, 16)
            sp.dma_start(xt_in[:, :, 2 * P:GROUP], x_t[0, :, :, 2 * P:GROUP]).then_inc(xt_loaded, 16)
            sp.dma_start(wvo_in[:], w_vo).then_inc(vo_loaded, 16)
            sp.dma_start(small_in[:], small).then_inc(small_loaded, 16)
            sp.dma_start(ctx_in[:, :, S:B * S], ctx_t[:, :, S:B * S]).then_inc(ctx_loaded[1], 16)
            sp.dma_start(w1_in[:], w1).then_inc(w1_loaded, 16)
            load_xt(1)
            sp.dma_start(w2_in[:], w2).then_inc(w2_loaded, 16)
            load_x(1)
            load_x(2)
            load_xt(2)
            sp.wait_ge(others_biased, 1)
            for b in range(1, B):
                for r in range(3):
                    sp.dma_start(stacked[32 * r:32 * (r + 1), b - 1, :],
                                 values[32 * (b - 1):32 * b, B + 1, :]).then_inc(rest_moved, 16)
            load_x(3)
            load_xt(3)
            store(0, 0)
            store(0, 1)
            with sp.Fori(4, GROUPS) as i:
                load_x(i)
                load_xt(i)
                store(i - 3, 0)
                store(i - 3, 1)
            with sp.Fori(GROUPS - 3, GROUPS - 1) as i:
                store(i, 0)
                store(i, 1)
            store(GROUPS - 1, 0)
            for t in range(2):
                sp.wait_ge(last_y_made, t + 1)
                sp.dma_start(out[GROUPS - 1, :, (2 + t) * D:(3 + t) * D], y[:, 2 + t, :]).then_inc(y_stored, 16)
            sp.wait_ge(y_stored, 16 * (2 * GROUPS + 1))

        @block.tensor
        def _(pe):
            mm = pe.matmul

            def warm_up():
                pe.wait_ge(vector_zeroed, 1)
                for _ in range(WARM_UPS):
                    mm(y_ps[0][:, 0:P], ones[:], ones[:], start=True, stop=True)

            def project_keys(h, m):
                lo, hi = PIECES[h]
                if h == 0 and m == 0:
                    pe.wait_ge(k_loaded, 16)
                if m == 0:
                    pe.wait_ge(ctx_loaded[h], 16)
                for k in range(KD):
                    last = mm(k_ps[h][m][:, 0:hi - lo], wk_t[:, k, m * P:(m + 1) * P], ctx_in[:, k, lo:hi],
                              start=k == 0, stop=k == KD - 1)
                last.then_inc(k_proj_ps_made, 1)

            def fold_keys(h, m):
                lo, hi = PIECES[h]
                if h == 1:
                    pe.wait_ge(vals_copied, 2)
                if h == 0:
                    pe.wait_ge(wq_step, 3 * KD)
                for k in range(KD):
                    pe.wait_ge(k_proj_made, KD * h + k + 1)
                    last = mm(key_ps[h][m][:, 0:hi - lo], wq[:, k, m * P:(m + 1) * P], k_proj[:, k, lo:hi],
                              start=k == 0, stop=k == KD - 1)
                last.then_inc(keys_ps_made, 1)

            def bias_scores(h):
                lo, hi = PIECES[h]
                if h == 0:
                    pe.wait_ge(wide_made, 1)
                else:
                    pe.wait_ge(sbias_made, 1)
                for k in range(KD):
                    last = mm(y_ps[1][:, 0:hi - lo], bq_wide[:, k, :], k_proj[:, k, lo:hi], start=k == 0, stop=k == KD - 1)
                last.then_inc(sbias_ps_made, 1)

            def fold_values(m):
                pe.wait_ge(vo_loaded, 16)
                for k in range(KD):
                    last = mm(z_ps[m][:, 0:D], wv[:, k, m * P:(m + 1) * P], wo_t[:, k, :], start=k == 0, stop=k == KD - 1)
                last.then_inc(wvo_ps_made, 1)

            def fold_value_bias():
                pe.wait_ge(wide_made, 2)
                for k in range(KD):
                    last = mm(y_ps[0][:, 0:D], bv_wide[:, k, :], wo_t[:, k, :], start=k == 0, stop=k == KD - 1)
                last.then_inc(wvo_ps_made, 1)

            def values_of(n):
                if n == 0:
                    pe.wait_ge(wvo_made, 2)
                    pe.wait_ge(rest_made, 3)
                elif n == 2:
                    pe.wait_ge(keys_hi_made, 2 * KD)
                elif n > 2:
                    pe.wait_ge(vals_copied, n - 1)
                if n == B + 1:
                    pe.wait_ge(rest_made, 4)
                batch = n - 1 if 1 < n <= B else 0
                for k in range(KD):
                    if n == 1:
                        rows = first_rest[:, k, :]
                    elif n == B + 1:
                        rows = other_rest[:, k, :]
                    else:
                        rows = ctx_in[:, k, batch * S:batch * S + P]
                    last = mm(z_ps[n % 2][:, 0:D], rows, wvo[:, k, :], start=k == 0, stop=k == KD - 1)
                last.then_inc(vals_ps_made, 1)

            def scores(n, p):
                if not above_zero(n):
                    pe.wait_ge(first_xt_lo_made, p + 1)
                elif p == 0:
                    pe.wait_ge(xt_lo_made, n)
                if above_zero(TILES * n + 2 * p):
                    pe.wait_ge(scaled_made, TILES * n + 2 * p)
                at = (n // PER_BATCH) * 2 * S
                for t in range(2):
                    rows = slice((2 * p + t) * P, (2 * p + t + 1) * P)
                    for k in range(KD):
                        if k > 0:
                            mm(sc_ps[t][:, 0:S], xt_lo[:, k, rows], keys[:, k, bass.ds(at, S)], start=False, stop=False)
                        last = mm(sc_ps[t][:, 0:2 * S], xt_hi[:, k, rows], keys[:, k, bass.ds(at, 2 * S)], start=k == 0,
                                  stop=k == KD - 1)
                        if k == 0:
                            mm(sc_ps[t][:, 0:S], xt_lo[:, k, rows], keys[:, k, bass.ds(at, S)], start=False, stop=False)
                last.then_inc(scores_made, 1)

            def transpose_picked(a, p):
                if isinstance(a, int) and a == 0 and p == 0:
                    pe.wait_ge(consts_made, 1)
                pe.wait_ge(rest_copied, 2 * a + p + 1)
                if above_zero(2 * (a - 1) + p + 1):
                    pe.wait_ge(x2nt_lo_made, 2 * (a - 1) + p + 1)
                for c in range(2):
                    for t in range(2):
                        last = pe.transpose(tr_ps[p][:, (2 * c + t) * P:(2 * c + t + 1) * P],
                                            picked[:, 2 * p + t, c * P:(c + 1) * P], ident[:])
                last.then_inc(pt_ps_made, 1)

            def attend(a, p):
                pe.wait_ge(pt_lo_made, 4 * a + 2 * p + 2)
                if p == 0:
                    pe.wait_ge(vals_lo_made, 2 if isinstance(a, int) and a < PER_BATCH else 4)
                    if above_zero(2 * (a - 1)):
                        pe.wait_ge(y_made, 2 * (a - 1))
                else:
                    pe.wait_ge(x2_made, TILES * a + 2)
                b = a // PER_BATCH
                for t in range(2):
                    dst = y_ps[0][:, t * D:(t + 1) * D]
                    rows = slice(t * P, (t + 1) * P)
                    hi, lo, rest = (v[:, bass.ds(b, 1), :].rearrange("p o d -> p (o d)") for v in (vals_hi, vals_lo, vals_rest))
                    mm(dst, pt_hi[:, 0, rows], hi, start=True, stop=False)
                    mm(dst, pt_hi[:, 0, rows], lo, start=False, stop=False)
                    mm(dst, pt_lo[:, rows], hi, start=False, stop=False)
                    last = mm(dst, pt_hi[0:96, 1, rows], rest[0:96], start=False, stop=True)
                last.then_inc(att_made, 1)

            def transpose_x2n(a, p):
                pe.wait_ge(x2n_made, TILES * a + 2 * p + 2)
                pe.wait_ge(pt_lo_made, 4 * a + 2 * p + 2)
                for k in range(KD):
                    for t in range(2):
                        last = pe.transpose(tr_ps[p][:, (2 * k + t) * P:(2 * k + t + 1) * P],
                                            x2n[:, 2 * p + t, k * P:(k + 1) * P], ident[:])
                last.then_inc(x2nt_ps_made, 1)

            def ffn_in(g, c, banks):
                if c == 0:
                    pe.wait_ge(x2nt_lo_made, 2 * g + 2)
                if above_zero(KF * g + c - len(banks) + 1):
                    pe.wait_ge(hid_made, KF * g + c - len(banks) + 1)
                dst = banks[c % len(banks)]
                cols = slice(c * P, (c + 1) * P)
                for k in range(KD):
                    mm(dst[:], w1_hi[:, k, cols], x2nt_hi[:, k, :], start=k == 0, stop=False)
                    mm(dst[:], w1_hi[:, k, cols], x2nt_lo[:, k, :], start=False, stop=False)
                    last = mm(dst[:], w1_lo[:, k, cols], x2nt_hi[:, k, :], start=False, stop=k == KD - 1)
                last.then_inc(z_made, 1)

            def ffn_out(a, g, j):
                if a is None and j == TILES - 1:
                    dst = tr_ps[0][:, 0:D]
                else:
                    dst = y_ps[1 - j // 2][:, (j % 2) * D:(j % 2 + 1) * D]
                rows = slice(j * P, (j + 1) * P)
                if j == 0:
                    if isinstance(g, int) and g == 0:
                        pe.wait_ge(w2_lo_made, 1)
                    if above_zero(2 * g - 1):
                        pe.wait_ge(y_made, 2 * g - 1)
                    pe.wait_ge(hid_hi_made, KF * g + KF - 1)
                if j == 2:
                    pe.wait_ge(x2_made, TILES * (g + 1 if a is None else a + 1))
                    if above_zero(2 * g):
                        pe.wait_ge(y_made, 2 * g)
                for c in range(KF):
                    if j == 0 and c == KF - 1:
                        pe.wait_ge(hid_hi_made, KF * g + KF)
                    mm(dst, hid_hi[:, c, rows], w2_hi[:, c, :], start=c == 0, stop=False)
                    mm(dst, hid_hi[:, c, rows], w2_lo[:, c, :], start=False, stop=False)
                for c in range(KF):
                    if j == 0 and c == 0:
                        pe.wait_ge(hid_lo_made, (KF - 1) * (g + 1))
                    if j == 0 and c == KF - 1:
                        pe.wait_ge(last_lo_made, g + 1)
                    last = mm(dst, hid_lo[:, c, rows], w2_hi[:, c, :], start=False, stop=c == KF - 1)
                last.then_inc(ffn_made, 1)

            def first_turn():
                fold_values(0)
                fold_values(1)
                fold_value_bias()
                values_of(0)
                values_of(1)
                scores(0, 1)
                project_keys(1, 0)
                transpose_picked(0, 0)
                project_keys(1, 1)
                fold_keys(1, 0)
                attend(0, 0)
                fold_keys(1, 1)
                transpose_picked(0, 1)
                bias_scores(1)
                attend(0, 1)
                scores(1, 0)
                transpose_x2n(0, 0)
                values_of(2)
                values_of(3)
                values_of(4)
                transpose_x2n(0, 1)
                values_of(5)
                scores(1, 1)
                pe.wait_ge(w1_lo_made, KD)
                pe.wait_ge(sbias_made, 2)
                pe.wait_ge(other_keys_lo_made, 1)
                pe.wait_ge(vals_copied, B + 2)

            def turn(a, g, n):
                if a is None and g is None:
                    scores(n, 0)
                    return
                if g is None:
                    first_turn()
                    return
                banks = last_z_ps if a is None else z_ps
                ffn_in(g, 0, banks)
                if a is not None and above_zero(g):
                    scores(a, 1)
                ffn_in(g, 1, banks)
                ffn_in(g, 2, banks)
                if a is not None:
                    transpose_picked(a, 0)
                ffn_in(g, 3, banks)
                ffn_in(g, 4, banks)
                if a is not None:
                    attend(a, 0)
                ffn_in(g, 5, banks)
                ffn_in(g, 6, banks)
                if a is not None:
                    transpose_picked(a, 1)
                ffn_in(g, 7, banks)
                ffn_out(a, g, 0)
                if a is not None:
                    attend(a, 1)
                ffn_out(a, g, 1)
                if n is not None:
                    scores(n, 0)
                if a is not None:
                    transpose_x2n(a, 0)
                ffn_out(a, g, 2)
                if a is not None:
                    transpose_x2n(a, 1)
                ffn_out(a, g, 3)

            warm_up()
            project_keys(0, 0)
            project_keys(0, 1)
            fold_keys(0, 0)
            fold_keys(0, 1)
            bias_scores(0)
            pe.wait_ge(keys_lo_made, KD)
            sweep(pe, turn)

        @block.scalar
        def _(act):
            func = act.activation
            act.dma_start(ctx_in[:, :, 0:S], ctx_t[:, :, 0:S]).then_inc(ctx_loaded[0], 16)

            def make_neg_half():
                act.wait_ge(vector_zeroed, 1)
                func(neg_half[:], ones[:, 0:TILES], ACT.Identity, scale=-0.5).then_inc(neg_half_made, 1)

            def widen_bq():
                act.wait_ge(q_loaded, 16)
                for k in range(KD):
                    last = func(bq_wide[:, k, :], ones[:], ACT.Identity, scale=bq[:, k, :])
                last.then_inc(wide_made, 1)

            def widen_bv():
                act.wait_ge(vo_loaded, 16)
                for k in range(KD):
                    last = func(bv_wide[:, k, :], ones[:], ACT.Identity, scale=bv[:, k, :])
                last.then_inc(wide_made, 1)

            def copy_k(h, m):
                lo, hi = PIECES[h]
                act.wait_ge(k_proj_ps_made, KD * h + m + 1)
                func(k_proj[:, m, lo:hi], k_ps[h][m][:, 0:hi - lo], ACT.Identity, bias=bk[:, m, :]).then_inc(k_proj_made, 1)

            def first_keys_to_hi():
                for m in range(KD):
                    act.wait_ge(keys_ps_made, m + 1)
                    func(keys[:, m, 0:S], tr_ps[m][:, 0:S], ACT.Copy).then_inc(keys_hi_made, 1)

            def other_keys_to_hi(m):
                act.wait_ge(keys_ps_made, KD + m + 1)
                func(keys_f32[:, m, :], z_ps[m][:, 0:(B - 1) * S], ACT.Copy).then_inc(keys_copied, 1)
                func(keys_by_batch[:, m, 1:B, 0, :], z_ps[m][:, 0:(B - 1) * S].rearrange("p (b s) -> p b s", s=S),
                     ACT.Copy).then_inc(keys_hi_made, 1)

            def copy_score_bias(h):
                lo, hi = PIECES[h]
                act.wait_ge(sbias_ps_made, h + 1)
                func(score_bias[:, lo:hi], y_ps[1][:, 0:hi - lo], ACT.Copy).then_inc(sbias_made, 1)

            def take_tanh():
                act.wait_ge(small_loaded, 16)
                func(tanh_g[:], small_in[:, 0:2], ACT.Tanh).then_inc(tanh_made, 1)

            def fold_wvo():
                act.wait_ge(tanh_made, 1)
                for m in range(KD):
                    act.wait_ge(wvo_ps_made, m + 1)
                    func(wvo[:, m, :], z_ps[m][:, 0:D], ACT.Identity, scale=tanh_g[:, 0:1]).then_inc(wvo_made, 1)

            def scale_bv():
                act.wait_ge(wvo_ps_made, 3)
                func(vo_part[:, 0, :], y_ps[0][:, 0:D], ACT.Identity, scale=tanh_g[:, 0:1]).then_inc(bv_scaled, 1)

            def copy_values(n):
                act.wait_ge(vals_ps_made, n + 1)
                func(values[:, n, :], z_ps[n % 2][:, 0:D], ACT.Copy).then_inc(vals_copied, 1)

            def first_values_to_hi():
                act.wait_ge(first_biased, 1)
                func(vals_hi[:, 0, :], values[:, 0, :], ACT.Copy).then_inc(vals_hi_made, 1)
                func(vals_rest[:, 0, :], values[:, 1, :], ACT.Copy).then_inc(vals_hi_made, 1)

            def other_values_to_hi():
                act.wait_ge(others_biased, 1)
                func(vals_hi[:, 1:B, :], values[:, 2:B + 1, :], ACT.Copy).then_inc(vals_hi_made, 1)
                act.wait_ge(rest_moved, 16 * 3 * (B - 1))
                func(vals_rest[0:96, 1:B, :], stacked[:], ACT.Copy).then_inc(vals_hi_made, 1)

            def w1_to_hi(k):
                act.wait_ge(w1_loaded, 16)
                func(w1_hi[:, k, :], w1_in[:, k, :], ACT.Copy).then_inc(w1_hi_made, 1)

            def w2_to_hi():
                act.wait_ge(w2_loaded, 16)
                func(w2_hi[:], w2_in[:], ACT.Identity, scale=tanh_g[:, 1:2]).then_inc(w2_hi_made, 1)

            def first_xt_to_hi(p):
                if p == 0:
                    act.wait_ge(first_xt_loaded, 16)
                else:
                    act.wait_ge(xt_loaded, 16)
                rows = slice(2 * p * P, 2 * (p + 1) * P)
                func(xt_hi[:, :, rows], xt_in[:, :, rows], ACT.Copy).then_inc(first_xt_hi_made, 1)

            def xt_to_hi(n):
                act.wait_ge(xt_loaded, 16 * (n + 1))
                act.wait_ge(scores_made, 2 * n)
                func(xt_hi[:], xt_in[:], ACT.Copy).then_inc(xt_hi_made, 1)

            def exps(a, p):
                for t in range(2):
                    j = 2 * p + t
                    act.wait_ge(topk_step, (2 * a + p) * STEPS + 3)
                    func(probs[:, j, :], score[:, j, :], ACT.Exp, bias=neg_max[:, j:j + 1], scale=SCALE).then_inc(probs_made, 1)

            def pt_to_hi(a, p):
                act.wait_ge(pt_ps_made, 2 * a + p + 1)
                if above_zero(2 * a + p):
                    act.wait_ge(att_made, 2 * a + p)
                func(pt_hi[:], tr_ps[p][:].rearrange("p (k c) -> p k c", k=2), ACT.Copy).then_inc(pt_hi_made, 1)

            def x2nt_to_hi(a, p):
                act.wait_ge(x2nt_ps_made, 2 * a + p + 1)
                func(x2nt_hi[:, :, 2 * p * P:2 * (p + 1) * P], tr_ps[p][:].rearrange("p (k c) -> p k c", k=KD),
                     ACT.Copy).then_inc(x2nt_hi_made, 1)

            def relu(g, c, banks):
                act.wait_ge(z_made, KF * g + c + 1)
                if c >= HID_RING:
                    act.wait_ge(hid_lo_made, (KF - 1) * g + c - HID_RING + 1)
                elif c < HID_RING - 1 and above_zero(g):
                    act.wait_ge(hid_lo_made, (KF - 1) * (g - 1) + c + KF - HID_RING + 1)
                elif above_zero(g):
                    act.wait_ge(last_lo_made, g)
                func(hid_hi[:, c, :], banks[c % len(banks)][:], ACT.Relu, bias=b1[:, c:c + 1]).then_inc(hid_hi_made, 1)
                func(hid[:, c % HID_RING, :], banks[c % len(banks)][:], ACT.Relu, bias=b1[:, c:c + 1]).then_inc(hid_made, 1)

            def first_turn():
                copy_score_bias(0)
                take_tanh()
                widen_bv()
                fold_wvo()
                scale_bv()
                exps(0, 0)
                w1_to_hi(0)
                copy_values(0)
                copy_values(1)
                w1_to_hi(1)
                copy_k(1, 0)
                pt_to_hi(0, 0)
                first_values_to_hi()
                copy_k(1, 1)
                exps(0, 1)
                xt_to_hi(1)
                other_keys_to_hi(0)
                pt_to_hi(0, 1)
                other_keys_to_hi(1)
                copy_score_bias(1)
                w2_to_hi()
                x2nt_to_hi(0, 0)
                copy_values(2)
                copy_values(3)
                copy_values(4)
                x2nt_to_hi(0, 1)
                copy_values(5)

            def turn(a, g, n):
                if a is None and g is None:
                    make_neg_half()
                    widen_bq()
                    copy_k(0, 0)
                    first_xt_to_hi(0)
                    copy_k(0, 1)
                    first_keys_to_hi()
                    first_xt_to_hi(1)
                    return
                if a is not None and g is None:
                    first_turn()
                    return
                if a is not None:
                    exps(a, 0)
                banks = last_z_ps if a is None else z_ps
                relu(g, 0, banks)
                if n is not None and above_zero(g):
                    xt_to_hi(n)
                relu(g, 1, banks)
                relu(g, 2, banks)
                if a is not None:
                    pt_to_hi(a, 0)
                    exps(a, 1)
                for c in range(3, 6):
                    relu(g, c, banks)
                if n is not None and not above_zero(g):
                    xt_to_hi(n)
                relu(g, 6, banks)
                if a is not None:
                    pt_to_hi(a, 1)
                relu(g, 7, banks)
                if isinstance(g, int) and g == 0:
                    other_values_to_hi()
                if a is not None:
                    x2nt_to_hi(a, 0)
                    x2nt_to_hi(a, 1)

            sweep(act, turn)

        @block.vector
        def _(dve):
            def prepare_keys():
                nc.vector.memset(ones[:], 1.0).then_inc(vector_zeroed, 1)
                dve.wait_ge(q_loaded, 16)
                for k in range(KD):
                    nc.vector.bn_stats(wq_stats[:, k, :], wq[:, k, :]).then_inc(wq_step, 1)
                for k in range(KD):
                    dve.wait_ge(wq_step, k + 1)
                    nc.vector.bn_aggr(wq_mean[:, k, :], wq_stats[:, k, :]).then_inc(wq_step, 1)
                for k in range(KD):
                    dve.wait_ge(wq_step, KD + k + 1)
                    nc.vector.tensor_scalar(wq[:, k, :], wq[:, k, :], wq_mean[:, k, 0:1], None, ALU.subtract).then_inc(wq_step, 1)

            def first_keys_to_lo():
                for m in range(KD):
                    dve.wait_ge(keys_hi_made, m + 1)
                    nc.vector.tensor_tensor(keys[:, m, S:2 * S], tr_ps[m][:, 0:S], keys[:, m, 0:S],
                                            ALU.subtract).then_inc(keys_lo_made, 1)

            def w2_to_lo():
                dve.wait_ge(w2_hi_made, 1)
                nc.vector.scalar_tensor_tensor(w2_lo[:], w2_in[:], tanh_g[:, 1:2], w2_hi[:], ALU.mult,
                                               ALU.subtract).then_inc(w2_lo_made, 1)

            def stats_x(n):
                dve.wait_ge(x_loaded, 16 * (n + 1))
                if above_zero(2 * n):
                    dve.wait_ge(norm1_step, 2 * n)
                apart(dve, vector_waited, n)
                for j in range(TILES):
                    rows = x_all[:, bass.ds(n, 1), j * D:(j + 1) * D].rearrange("p o d -> p (o d)")
                    nc.vector.bn_stats(stats1[:, j, :], rows).then_inc(stats1_step, 1)
                for j in range(TILES):
                    dve.wait_ge(stats1_step, 2 * TILES * n + j + 1)
                    apart(dve, vector_waited, n)
                    nc.vector.bn_aggr(mv1[:, j, :], stats1[:, j, :]).then_inc(stats1_step, 1)

            def first_xt_to_lo(p):
                dve.wait_ge(first_xt_hi_made, p + 1)
                rows = slice(2 * p * P, 2 * (p + 1) * P)
                nc.vector.tensor_tensor(xt_lo[:, :, rows], xt_in[:, :, rows], xt_hi[:, :, rows],
                                        ALU.subtract).then_inc(first_xt_lo_made, 1)

            def scale_scores(a, p):
                at = (a // PER_BATCH) * S
                dve.wait_ge(scores_made, 2 * a + p + 1)
                if p == 0:
                    dve.wait_ge(norm1_step, 2 * (a + 1))
                for t in range(2):
                    j = 2 * p + t
                    if above_zero(TILES * (a - 1) + j + 1):
                        dve.wait_ge(probs_made, TILES * (a - 1) + j + 1)
                    nc.vector.scalar_tensor_tensor(score[:, j, :], sc_ps[t][:, S:2 * S], norm1[:, 1, j:j + 1],
                                                   score_bias[:, bass.ds(at, S)], ALU.mult, ALU.add).then_inc(scaled_part, 1)
                for t in range(2):
                    j = 2 * p + t
                    dve.wait_ge(scaled_part, TILES * a + j + 1)
                    apart(dve, vector_waited, a)
                    nc.vector.scalar_tensor_tensor(score[:, j, :], sc_ps[t][:, 0:S], norm1[:, 1, j:j + 1],
                                                   score[:, j, :], ALU.mult, ALU.add).then_inc(scaled_made, 1)

            def topk_round(a, p, r):
                done = (2 * a + p) * STEPS
                at = 0 if r == 0 else 4 * r + 1
                for t in range(2):
                    j = 2 * p + t
                    if r == 0:
                        dve.wait_ge(scaled_made, TILES * a + j + 1)
                    else:
                        dve.wait_ge(topk_step, done + at - 1 + t)
                    apart(dve, vector_waited, a)
                    nc.vector.max(top[:, j, 8 * r:8 * r + 8], score[:, j, :] if r == 0 else left[:, j, :]).then_inc(topk_step, 1)
                if r == 0:
                    dve.wait_ge(topk_step, done + 2)
                    nc.vector.tensor_scalar(neg_max[:, 2 * p:2 * p + 2], top[:, 2 * p:2 * p + 2, 0], -SCALE, None,
                                            ALU.mult).then_inc(topk_step, 1)
                for t in range(2):
                    j = 2 * p + t
                    dve.wait_ge(topk_step, done + at + 1 + t)
                    apart(dve, vector_waited, a)
                    nc.vector.match_replace(left[:, j, :], top[:, j, 8 * r:8 * r + 8], score[:, j, :] if r == 0 else left[:, j, :],
                                            TAKEN).then_inc(topk_step, 1)

            def pick(a, p):
                for t in range(2):
                    j = 2 * p + t
                    dve.wait_ge(topk_step, (2 * a + p) * STEPS + STEPS - 1 + t)
                    dve.wait_ge(probs_made, TILES * a + j + 1)
                    nc.vector.scalar_tensor_tensor(picked[:, j, 0:S], left[:, j, :], TAKEN, probs[:, j, :], ALU.is_equal, ALU.mult,
                                                   accum_out=denom[:, j:j + 1]).then_inc(picked_made, 1)

            def copy_rest(a, p):
                dve.wait_ge(picked_made, TILES * a + 2 * p + 2)
                if isinstance(a, int) and a == 0 and p == 0:
                    dve.wait_ge(pool_zeroed, 4)
                rest = picked[:, 2 * p:2 * p + 2, P:2 * P].rearrange("p j (r c) -> p j r c", c=32)
                nc.vector.tensor_copy(rest[:, :, 1:3, 0:SR], rest[:, :, 0:1, 0:SR].to_broadcast([P, 2, 2, SR])).then_inc(rest_copied, 1)

            def invert(a, p):
                dve.wait_ge(picked_made, TILES * a + 2 * p + 2)
                nc.vector.reciprocal(inv_denom[:, 2 * p:2 * p + 2], denom[:, 2 * p:2 * p + 2]).then_inc(inv_made, 1)

            def pt_to_lo(a, p):
                dve.wait_ge(pt_hi_made, 2 * a + p + 1)
                nc.vector.tensor_tensor(pt_lo[:], tr_ps[p][:, 0:2 * P], pt_hi[:, 0, :], ALU.subtract).then_inc(pt_lo_made, 1)
                nc.vector.tensor_tensor(pt_hi[32:64, 1, :], tr_ps[p][32:64, 2 * P:4 * P], pt_hi[32:64, 1, :],
                                        ALU.subtract).then_inc(pt_lo_made, 1)

            def residual(a, p):
                dve.wait_ge(att_made, 2 * a + p + 1)
                dve.wait_ge(inv_made, 2 * a + p + 1)
                if above_zero(2 * (a - 1) + p + 1):
                    dve.wait_ge(x2b_made, 2 * (a - 1) + p + 1)
                apart(dve, vector_waited, a)
                for t in range(2):
                    j = 2 * p + t
                    rows = x_all[:, bass.ds(a, 1), j * D:(j + 1) * D].rearrange("p o d -> p (o d)")
                    nc.vector.scalar_tensor_tensor(x2[:, j, :], y_ps[0][:, t * D:(t + 1) * D], inv_denom[:, j:j + 1], rows,
                                                   ALU.mult, ALU.add).then_inc(x2_made, 1)
                for t in range(2):
                    j = 2 * p + t
                    dve.wait_ge(x2_made, TILES * a + j + 1)
                    nc.vector.bn_stats(stats2[:, j, :], x2[:, j, :]).then_inc(stats2_step, 1)
                for t in range(2):
                    j = 2 * p + t
                    dve.wait_ge(stats2_step, 2 * TILES * a + 4 * p + t + 1)
                    apart(dve, vector_waited, a)
                    nc.vector.bn_aggr(mv2[:, j, :], stats2[:, j, :]).then_inc(stats2_step, 1)

            def x2nt_to_lo(a, p):
                dve.wait_ge(x2nt_hi_made, 2 * a + p + 1)
                cols = slice(2 * p * P, 2 * (p + 1) * P)
                nc.vector.tensor_tensor(x2nt_lo[:, :, cols], tr_ps[p][:].rearrange("p (k c) -> p k c", k=KD),
                                        x2nt_hi[:, :, cols], ALU.subtract).then_inc(x2nt_lo_made, 1)

            def last_hid_to_lo(g):
                dve.wait_ge(hid_hi_made, KF * g + KF)
                dve.wait_ge(hid_made, KF * g + KF)
                if above_zero(TILES * g):
                    dve.wait_ge(ffn_made, TILES * g)
                nc.vector.tensor_tensor(hid_lo[:, KF - 1, :], hid[:, (KF - 1) % HID_RING, :], hid_hi[:, KF - 1, :],
                                        ALU.subtract).then_inc(last_lo_made, 1)

            def output(g, p):
                dve.wait_ge(ffn_made, TILES * g + 2 * p + 2)
                dve.wait_ge(x2b_made, 2 * g + 2)
                if above_zero(32 * g):
                    dve.wait_ge(y_stored, 32 * g)
                nc.vector.tensor_tensor(y[:, 2 * p:2 * p + 2, :], y_ps[1 - p][:].rearrange("p (j d) -> p j d", j=2),
                                        x2b[:, 2 * p:2 * p + 2, :], ALU.add).then_inc(y_made, 1)

            def first_turn():
                scale_scores(0, 0)
                for r in range(ROUNDS):
                    topk_round(0, 0, r)
                pick(0, 0)
                copy_rest(0, 0)
                invert(0, 0)
                scale_scores(0, 1)
                topk_round(0, 1, 0)
                pt_to_lo(0, 0)
                for r in range(1, ROUNDS):
                    topk_round(0, 1, r)
                pick(0, 1)
                copy_rest(0, 1)
                invert(0, 1)
                residual(0, 0)
                pt_to_lo(0, 1)
                stats_x(1)
                residual(0, 1)
                scale_scores(1, 0)
                x2nt_to_lo(0, 0)
                topk_round(1, 0, 0)
                x2nt_to_lo(0, 1)
                dve.wait_ge(sbias_made, 2)

            def last_outputs():
                g = GROUPS - 1
                dve.wait_ge(x2b_made, 2 * g + 2)
                dve.wait_ge(y_stored, 32 * g)
                for t in range(2):
                    dve.wait_ge(ffn_made, TILES * g + 2 + t + 1)
                    nc.vector.tensor_tensor(y[:, 2 + t, :], (y_ps[0], tr_ps[0])[t][:, 0:D], x2b[:, 2 + t, :],
                                            ALU.add).then_inc(last_y_made, 1)

            def turn(a, g, n):
                if a is None and g is None:
                    first_xt_to_lo(0)
                    stats_x(n)
                    first_keys_to_lo()
                    first_xt_to_lo(1)
                    dve.wait_ge(sbias_made, 1)
                    return
                if a is not None and g is None:
                    first_turn()
                    return
                if a is not None and above_zero(g):
                    scale_scores(a, 0)
                    topk_round(a, 0, 0)
                if above_zero(g):
                    x2nt_to_lo(g, 1)
                if a is not None:
                    topk_round(a, 0, 1)
                    topk_round(a, 0, 2)
                if above_zero(g):
                    output(g - 1, 1)
                if a is not None:
                    topk_round(a, 0, 3)
                    pick(a, 0)
                    copy_rest(a, 0)
                    invert(a, 0)
                    scale_scores(a, 1)
                    topk_round(a, 1, 0)
                    topk_round(a, 1, 1)
                    pt_to_lo(a, 0)
                    topk_round(a, 1, 2)
                    topk_round(a, 1, 3)
                    pick(a, 1)
                    copy_rest(a, 1)
                    invert(a, 1)
                    if isinstance(g, int) and g == 0:
                        w2_to_lo()
                    residual(a, 0)
                    pt_to_lo(a, 1)
                last_hid_to_lo(g)
                if n is not None:
                    stats_x(n)
                if a is not None:
                    residual(a, 1)
                output(g, 0)
                if a is not None:
                    x2nt_to_lo(a, 0)
                else:
                    last_outputs()

            prepare_keys()
            sweep(dve, turn)

        @block.gpsimd
        def _(pool):
            def prepare():
                nc.gpsimd.memset(ident[:], 0.0).then_inc(pool_zeroed, 1)
                nc.gpsimd.memset(first_rest[:], 0.0).then_inc(pool_zeroed, 1)
                nc.gpsimd.memset(other_rest[:], 0.0).then_inc(pool_zeroed, 1)
                nc.gpsimd.memset(picked[:], 0.0).then_inc(pool_zeroed, 1)
                pool.wait_ge(pool_zeroed, 4)
                nc.gpsimd.affine_select(out=ident[:], in_=ident[:], compare_op=ALU.not_equal, fill=1.0, base=0,
                                        pattern=[[-1, P]], channel_multiplier=1).then_inc(consts_made, 1)

            def stack_first_rest():
                pool.wait_ge(ctx_loaded[0], 16)
                for r in range(3):
                    for k in range(KD):
                        last = nc.gpsimd.tensor_copy(first_rest[:, k, 32 * r:32 * r + SR], ctx_in[:, k, P:S])
                    last.then_inc(rest_made, 1)

            def place_other_rests():
                pool.wait_ge(ctx_loaded[1], 16)
                for k in range(KD):
                    last = nc.gpsimd.tensor_copy(other_rest[:, k, 0:32 * (B - 1)].rearrange("p (b s) -> p b s", s=32)[:, :, 0:SR],
                                                 ctx_in[:, k, S:B * S].rearrange("p (b s) -> p b s", s=S)[:, :, P:S])
                last.then_inc(rest_made, 1)

            def other_keys_to_lo():
                pool.wait_ge(keys_copied, KD)
                pool.wait_ge(keys_hi_made, 2 * KD)
                nc.gpsimd.tensor_tensor(keys_by_batch[:, :, 1:B, 1, :], keys_f32[:].rearrange("p k (b s) -> p k b s", s=S),
                                        keys_by_batch[:, :, 1:B, 0, :], ALU.subtract).then_inc(other_keys_lo_made, 1)

            def scale_bo():
                pool.wait_ge(tanh_made, 1)
                nc.gpsimd.tensor_scalar(vo_part[:, 1, :], bo, tanh_g[:, 0:1], 1.0, ALU.mult, ALU.mult).then_inc(bo_scaled, 1)

            def add_value_bias():
                pool.wait_ge(bo_scaled, 1)
                pool.wait_ge(bv_scaled, 1)
                nc.gpsimd.tensor_tensor(vo_bias[:], vo_part[:, 0, :], vo_part[:, 1, :], ALU.add).then_inc(vo_bias_made, 1)
                pool.wait_ge(vo_bias_made, 1)
                pool.wait_ge(vals_copied, 2)
                wide = vo_bias[:].unsqueeze(1).to_broadcast([P, 2, D])
                nc.gpsimd.tensor_tensor(values[:, 0:2, :], values[:, 0:2, :], wide, ALU.add).then_inc(first_biased, 1)

            def bias_other_values():
                pool.wait_ge(vals_copied, B + 2)
                wide = vo_bias[:].unsqueeze(1).to_broadcast([P, B, D])
                nc.gpsimd.tensor_tensor(values[:, 2:B + 2, :], values[:, 2:B + 2, :], wide, ALU.add).then_inc(others_biased, 1)

            def first_values_to_lo():
                pool.wait_ge(vals_hi_made, 2)
                nc.gpsimd.tensor_tensor(vals_lo[:, 0, :], values[:, 0, :], vals_hi[:, 0, :], ALU.subtract).then_inc(vals_lo_made, 1)
                pool.wait_ge(vals_lo_made, 1)
                nc.gpsimd.tensor_tensor(vals_rest[64:96, 0, :], values[64:96, 1, :], vals_rest[64:96, 0, :],
                                        ALU.subtract).then_inc(vals_lo_made, 1)
                pool.wait_ge(vals_lo_made, 2)

            def other_values_to_lo():
                pool.wait_ge(vals_hi_made, 4)
                nc.gpsimd.tensor_tensor(vals_lo[:, 1:B, :], values[:, 2:B + 1, :], vals_hi[:, 1:B, :],
                                        ALU.subtract).then_inc(vals_lo_made, 1)
                pool.wait_ge(vals_lo_made, 3)
                nc.gpsimd.tensor_tensor(vals_rest[64:96, 1:B, :], stacked[64:96], vals_rest[64:96, 1:B, :],
                                        ALU.subtract).then_inc(vals_lo_made, 1)
                pool.wait_ge(vals_lo_made, 4)

            def w1_to_lo(k):
                pool.wait_ge(w1_hi_made, k + 1)
                nc.gpsimd.tensor_tensor(w1_lo[:, k, :], w1_in[:, k, :], w1_hi[:, k, :], ALU.subtract).then_inc(w1_lo_made, 1)

            def scale_b2():
                pool.wait_ge(tanh_made, 1)
                for t in range(2):
                    nc.gpsimd.tensor_scalar(b2_pair[:, t, :], b2, tanh_g[:, 1:2], 1.0, ALU.mult, ALU.mult).then_inc(b2_made, 1)

            def xt_to_lo(n):
                pool.wait_ge(xt_hi_made, n)
                nc.gpsimd.tensor_tensor(xt_lo[:], xt_in[:], xt_hi[:], ALU.subtract).then_inc(xt_lo_made, 1)

            def rstd_x(n):
                if not above_zero(n):
                    pool.wait_ge(neg_half_made, 1)
                pool.wait_ge(stats1_step, 2 * TILES * (n + 1))
                if above_zero(TILES * n):
                    pool.wait_ge(scaled_made, TILES * n)
                apart(pool, pool_waited, n)
                nc.gpsimd.tensor_scalar(norm1[:, 0, :], mv1[:, :, 1], EPS, 1.0, ALU.add, ALU.mult).then_inc(norm1_step, 1)
                pool.wait_ge(norm1_step, 2 * n + 1)
                nc.gpsimd.tensor_tensor(norm1[:, 1, :], norm1[:, 0, :], neg_half[:], ALU.pow).then_inc(norm1_step, 1)

            def normalise_x2(a, p):
                cols = slice(2 * p, 2 * p + 2)
                pool.wait_ge(stats2_step, 2 * TILES * a + 4 * p + 4)
                apart(pool, pool_waited, a)
                nc.gpsimd.tensor_scalar(norm2[:, 0, cols], mv2[:, cols, 1], EPS, 1.0, ALU.add, ALU.mult).then_inc(norm2_step, 1)
                nc.gpsimd.tensor_scalar(norm2[:, 1, cols], mv2[:, cols, 0], -1.0, 0.0, ALU.mult, ALU.add).then_inc(norm2_step, 1)
                pool.wait_ge(norm2_step, 6 * a + 3 * p + 1)
                nc.gpsimd.tensor_tensor(norm2[:, 2, cols], norm2[:, 0, cols], neg_half[:, 0:2], ALU.pow).then_inc(norm2_step, 1)
                pool.wait_ge(norm2_step, 6 * a + 3 * p + 3)
                if above_zero(2 * (a - 1) + p + 1):
                    pool.wait_ge(x2nt_ps_made, 2 * (a - 1) + p + 1)
                apart(pool, pool_waited, a)
                for t in range(2):
                    j = 2 * p + t
                    nc.gpsimd.tensor_scalar(x2n[:, j, :], x2[:, j, :], norm2[:, 1, j:j + 1], norm2[:, 2, j:j + 1],
                                            ALU.add, ALU.mult).then_inc(x2n_made, 1)

            def add_b2(g, p):
                if above_zero(2 * (g - 1) + p + 1):
                    pool.wait_ge(y_made, 2 * (g - 1) + p + 1)
                pool.wait_ge(x2_made, TILES * g + 2 * p + 2)
                if not above_zero(g) and p == 0:
                    pool.wait_ge(b2_made, 2)
                pair = slice(2 * p, 2 * p + 2)
                nc.gpsimd.tensor_tensor(x2b[:, pair, :], x2[:, pair, :], b2_pair[:], ALU.add).then_inc(x2b_made, 1)

            def hid_to_lo(g, c):
                pool.wait_ge(hid_hi_made, KF * g + c + 1)
                pool.wait_ge(hid_made, KF * g + c + 1)
                if above_zero(TILES * g):
                    pool.wait_ge(ffn_made, TILES * g)
                nc.gpsimd.tensor_tensor(hid_lo[:, c, :], hid[:, c % HID_RING, :], hid_hi[:, c, :], ALU.subtract).then_inc(hid_lo_made, 1)

            def first_turn():
                place_other_rests()
                scale_b2()
                add_value_bias()
                w1_to_lo(0)
                first_values_to_lo()
                w1_to_lo(1)
                xt_to_lo(1)
                normalise_x2(0, 0)
                rstd_x(1)
                normalise_x2(0, 1)
                other_keys_to_lo()
                bias_other_values()
                add_b2(0, 0)

            def turn(a, g, n):
                if a is None and g is None:
                    rstd_x(n)
                    stack_first_rest()
                    scale_bo()
                    return
                if a is not None and g is None:
                    first_turn()
                    return
                add_b2(g, 1)
                for c in range(KF - 1):
                    hid_to_lo(g, c)
                if n is not None:
                    xt_to_lo(n)
                if a is not None:
                    normalise_x2(a, 0)
                if n is not None:
                    rstd_x(n)
                if a is not None:
                    normalise_x2(a, 1)
                    add_b2(a, 0)
                if isinstance(g, int) and g == 0:
                    other_values_to_lo()

            prepare()
            sweep(pool, turn)


def kernel(x, ctx_1024, g_xattn, g_ffn, L0_xattn_Wq, L0_xattn_bq, L0_xattn_Wk, L0_xattn_bk, L0_xattn_Wv, L0_xattn_bv,
           L0_xattn_Wo, L0_xattn_bo, L0_ffn_W1, L0_ffn_b1, L0_ffn_W2, L0_ffn_b2):
    import numpy as np
    import concourse.bacc as bacc
    from concourse.bass_utils import run_bass_kernel_spmd

    def by_partition(a):
        a = np.asarray(a)
        return a.reshape(-1, P, a.shape[-1]).transpose(1, 0, 2)

    def column(v):
        return by_partition(np.asarray(v)[:, None])

    def everywhere(v):
        v = np.asarray(v)
        return np.broadcast_to(v, (P, v.size))

    ctx_rows = np.asarray(ctx_1024).reshape(B * S, D)
    arrays = {
        "x": np.asarray(x).reshape(GROUPS, P, TILES * D),
        "x_t": np.asarray(x).reshape(GROUPS, P, TILES, KD, P).transpose(0, 4, 3, 2, 1).reshape(GROUPS, P, KD, GROUP),
        "w_k": np.concatenate([by_partition(np.asarray(L0_xattn_Wk).T), column(L0_xattn_bk)], axis=2),
        "w_q": np.concatenate([by_partition(L0_xattn_Wq), column(L0_xattn_bq)], axis=2),
        "ctx_t": by_partition(ctx_rows.T),
        "w_vo": np.concatenate([by_partition(L0_xattn_Wv), by_partition(np.asarray(L0_xattn_Wo).T), column(L0_xattn_bv)], axis=2),
        "small": np.concatenate([everywhere(g_xattn), everywhere(g_ffn), np.asarray(L0_ffn_b1).reshape(KF, P).T,
                                 everywhere(L0_xattn_bo), everywhere(L0_ffn_b2)], axis=1),
        "w1": by_partition(L0_ffn_W1),
        "w2": by_partition(L0_ffn_W2),
    }
    arrays = {k: np.ascontiguousarray(v) for k, v in arrays.items()}
    nc = bacc.Bacc("TRN2", target_bir_lowering=False, num_devices=1)
    args = [nc.dram_tensor(k, v.shape, mybir.dt.float32, kind="ExternalInput").ap() for k, v in arrays.items()]
    out = nc.dram_tensor("out", (GROUPS, P, TILES * D), mybir.dt.float32, kind="ExternalOutput").ap()
    gated_block(nc, *args, out)
    r = run_bass_kernel_spmd(nc, [arrays], core_ids=[0])
    return r.results[0]["out"].reshape(B, T, D)
```
